# Optimizing a Trainium2 kernel written in Bass

```python
import numpy as np
import jax
import jax.numpy as jnp

def _softmax(x, axis=-1):
    return jax.nn.softmax(x, axis=axis)

def _gelu(x):
    return jax.nn.gelu(x, approximate=True)

def _silu(x):
    return jax.nn.silu(x)

def _sigmoid(x):
    return jax.nn.sigmoid(x)

def _layernorm(x, axis=-1, eps=1e-05):
    m = jnp.mean(x, axis=axis, keepdims=True)
    v = jnp.var(x, axis=axis, keepdims=True)
    return (x - m) / jnp.sqrt(v + eps)

def _scatter_add(tgt, idx, src, axis=0):
    return tgt.at[idx].add(src)

def _segment_sum(src, seg, n):
    return jax.ops.segment_sum(src, seg, n)
kernel_name = 'mk_adj_preln_d2_adj_r2_726514'

def setup_inputs(seed: int=0):
    np.random.seed(seed)
    _w = jnp.asarray

    def _rec_inputs():
        import jax
        import jax.numpy as jnp
        _gk = jax.random.key(seed)
        x = 7.22e-05 + 1 * jax.random.normal(jax.random.fold_in(_gk, 1), (128, 128, 256), jnp.float32)
        _w = (1.0 + jnp.arange(128, dtype=jnp.float32)) ** (-0.5)
        _w = _w / _w.mean()
        _pij = jnp.clip(0.03125 * _w[:, None] * _w[None, :], 0.0, 1.0)
        _a = jax.random.uniform(jax.random.fold_in(_gk, 2), (128, 128, 128)) < _pij
        adj = _a.astype(jnp.int32)
        return (x, adj)
    x, adj = _rec_inputs()

    def _L0_gnn_setup():
        import jax, jax.numpy as jnp
        import numpy as np
        ALPHA = 0.2
        NEG_INF = -1000000000.0
        key = jax.random.key(seed)
        k1, k2, k3, k4 = jax.random.split(key, 4)
        B, N, IN, OUT = (8, 1024, 256, 32)
        graph_input = jax.random.normal(k1, (B, N, IN), dtype=jnp.float32)
        adj = jax.random.randint(k2, (B, N, N), 0, 2, dtype=jnp.int32)
        W_fc = jax.random.normal(k3, (OUT, IN), dtype=jnp.float32) * (1.0 / np.sqrt(IN))
        W_attn = jax.random.normal(k4, (1, 2 * OUT), dtype=jnp.float32) * (1.0 / np.sqrt(2 * OUT))
        return {'graph_input': graph_input, 'adj': adj, 'W_fc': W_fc, 'W_attn': W_attn}
    _L0_gnn_all = _L0_gnn_setup()
    _L0_gnn_in = {k: v for k, v in _L0_gnn_all.items() if k in ('W_fc', 'W_attn')}
    del _L0_gnn_all

    def _L1_gnn_setup():
        import jax, jax.numpy as jnp
        import numpy as np
        L = 3
        D = 256
        B, N = (8, 512)
        EPS = 1e-05

        def layernorm(x, gamma, beta):
            mu = jnp.mean(x, axis=-1, keepdims=True)
            var = jnp.var(x, axis=-1, keepdims=True)
            return (x - mu) * jax.lax.rsqrt(var + EPS) * gamma + beta
        key = jax.random.key(seed)
        ks = jax.random.split(key, 12)
        s = 1.0 / np.sqrt(D)
        node_features = jax.random.normal(ks[0], (B, N, D), dtype=jnp.float32)
        adjacency_matrix = jax.random.randint(ks[1], (B, N, N), 0, 2, dtype=jnp.int32)
        return {'node_features': node_features, 'adjacency_matrix': adjacency_matrix, 'attn_w': jax.random.normal(ks[2], (L, 2 * D), dtype=jnp.float32) * (1.0 / np.sqrt(2 * D)), 'attn_b': jax.random.normal(ks[3], (L,), dtype=jnp.float32) * 0.01, 'W1': jax.random.normal(ks[4], (L, D, 4 * D), dtype=jnp.float32) * s, 'b1': jnp.zeros((L, 4 * D), dtype=jnp.float32), 'W2': jax.random.normal(ks[5], (L, 4 * D, D), dtype=jnp.float32) * (1.0 / np.sqrt(4 * D)), 'b2': jnp.zeros((L, D), dtype=jnp.float32), 'g1': jnp.ones((L, D), dtype=jnp.float32), 'beta1': jnp.zeros((L, D), dtype=jnp.float32), 'g2': jnp.ones((L, D), dtype=jnp.float32), 'beta2': jnp.zeros((L, D), dtype=jnp.float32)}
    _L1_gnn_all = _L1_gnn_setup()
    _L1_gnn_in = {k: v for k, v in _L1_gnn_all.items() if k in ('attn_w', 'attn_b', 'W1', 'b1', 'W2', 'b2', 'g1', 'beta1', 'g2', 'beta2')}
    del _L1_gnn_all
    return {'x': x, 'adj': adj, 'L0_gnn_W_fc': _L0_gnn_in['W_fc'], 'L0_gnn_W_attn': _L0_gnn_in['W_attn'], 'L1_gnn_attn_w': _L1_gnn_in['attn_w'], 'L1_gnn_attn_b': _L1_gnn_in['attn_b'], 'L1_gnn_W1': _L1_gnn_in['W1'], 'L1_gnn_b1': _L1_gnn_in['b1'], 'L1_gnn_W2': _L1_gnn_in['W2'], 'L1_gnn_b2': _L1_gnn_in['b2'], 'L1_gnn_g1': _L1_gnn_in['g1'], 'L1_gnn_beta1': _L1_gnn_in['beta1'], 'L1_gnn_g2': _L1_gnn_in['g2'], 'L1_gnn_beta2': _L1_gnn_in['beta2']}

def reference(x, adj, L0_gnn_W_fc, L0_gnn_W_attn, L1_gnn_attn_w, L1_gnn_attn_b, L1_gnn_W1, L1_gnn_b1, L1_gnn_W2, L1_gnn_b2, L1_gnn_g1, L1_gnn_beta1, L1_gnn_g2, L1_gnn_beta2):
    import jax
    import jax.numpy as jnp

    def _L0_gnn_ref(graph_input, adj, W_fc, W_attn):
        import jax, jax.numpy as jnp
        import numpy as np
        ALPHA = 0.2
        NEG_INF = -1000000000.0
        h = jnp.einsum('bni,oi->bno', graph_input, W_fc)
        out_dim = W_fc.shape[0]
        a1 = W_attn[0, :out_dim]
        a2 = W_attn[0, out_dim:]
        f1 = jnp.einsum('bno,o->bn', h, a1)
        f2 = jnp.einsum('bno,o->bn', h, a2)
        scores = jax.nn.leaky_relu(f1[:, :, None] + f2[:, None, :], negative_slope=ALPHA)
        scores = jnp.where(adj == 0, NEG_INF, scores)
        attn = jax.nn.softmax(scores, axis=2)
        h_prime = jnp.einsum('bnm,bmi->bni', attn, graph_input)
        return jax.nn.elu(h_prime)

    def _L1_gnn_ref(node_features, adjacency_matrix, attn_w, attn_b, W1, b1, W2, b2, g1, beta1, g2, beta2):
        import jax, jax.numpy as jnp
        import numpy as np
        L = 3
        D = 256
        B, N = (8, 512)
        EPS = 1e-05

        def layernorm(x, gamma, beta):
            mu = jnp.mean(x, axis=-1, keepdims=True)
            var = jnp.var(x, axis=-1, keepdims=True)
            return (x - mu) * jax.lax.rsqrt(var + EPS) * gamma + beta
        n = adjacency_matrix.shape[-1]
        mask = adjacency_matrix.astype(jnp.float32) + jnp.eye(n, dtype=jnp.float32) > 0
        x = node_features
        d = x.shape[-1]
        for l in range(attn_w.shape[0]):
            si = x @ attn_w[l, :d]
            sj = x @ attn_w[l, d:]
            scores = si[:, :, None] + sj[:, None, :] + attn_b[l]
            scores = jnp.where(scores >= 0, scores, 0.2 * scores)
            scores = jnp.where(mask, scores, -jnp.inf)
            attn = jax.nn.softmax(scores, axis=-1)
            agg = jnp.einsum('bij,bjd->bid', attn, x)
            h = layernorm(x + agg, g1[l], beta1[l])
            ff = jax.nn.gelu(h @ W1[l] + b1[l], approximate=False) @ W2[l] + b2[l]
            x = layernorm(h + ff, g2[l], beta2[l])
        return x
    h = jnp.maximum(_layernorm(x, axis=-1), 0.0)
    x = x + _L0_gnn_ref(h, adj, L0_gnn_W_fc, L0_gnn_W_attn)
    h = jnp.maximum(_layernorm(x, axis=-1), 0.0)
    x = x + _L1_gnn_ref(h, adj, L1_gnn_attn_w, L1_gnn_attn_b, L1_gnn_W1, L1_gnn_b1, L1_gnn_W2, L1_gnn_b2, L1_gnn_g1, L1_gnn_beta1, L1_gnn_g2, L1_gnn_beta2)
    return x

_drawn_inputs = setup_inputs


def setup_inputs(seed=0):
    import zlib

    import numpy as np

    out = dict(_drawn_inputs(seed))
    spreads = {'L1_gnn_b1': (0.0, 0.1),
     'L1_gnn_b2': (0.0, 0.1),
     'L1_gnn_g1': (1.0, 0.2),
     'L1_gnn_beta1': (0.0, 0.1),
     'L1_gnn_g2': (1.0, 0.2),
     'L1_gnn_beta2': (0.0, 0.1)}
    factors = {'L1_gnn_attn_b': 64.0}
    for name, (base, spread) in spreads.items():
        noise = np.random.default_rng([zlib.crc32(name.encode()), seed]).standard_normal(out[name].shape)
        drawn = base * np.exp(spread * noise) if base else spread * noise
        out[name] = jnp.asarray(drawn.astype(out[name].dtype))
    for name, factor in factors.items():
        out[name] = (out[name] * factor).astype(out[name].dtype)
    return out
```

```python
from contextlib import ExitStack

import concourse.bass as bass
from concourse import mybir

ALU = mybir.AluOpType
ACT = mybir.ActivationFunctionType
AX = mybir.AxisListType.X
F32 = mybir.dt.float32
F32R = mybir.dt.float32r
BF16 = mybir.dt.bfloat16
I32 = mybir.dt.int32

P = 128
T = 4
EPS = 1e-5
SLOPE = 0.2
BIG = 2.0 ** 100


class Step:

    def __init__(self, s, off=0):
        self.s, self.off = s, off

    def nth(self, unit, per=1, j=None):
        return unit * per + (per if j is None else j) + self.off * per


def build(nc, x, adj, w_fc, w_attn0, attn_w, attn_b, w1, b1, w2, b2, g1, beta1, g2, beta2, out):
    B, N, D = x.shape
    L = w1.shape[0]
    F = w1.shape[2]
    O = w_fc.shape[0]
    K1 = D // P
    C = F // P
    G = B // T
    U = L * G
    assert N == P and K1 == 2 and C == 8

    x_u = x.rearrange("(g t) n d -> g n t d", t=T)
    adj_u = adj.rearrange("(g t) n m -> g n t m", t=T)
    out_u = out.rearrange("(g t) n d -> g n t d", t=T)
    y_u = nc.dram_tensor("y_scratch", (max(L - 1, 1) * G, P, T, D), F32, kind="Internal").ap()
    r_u = nc.dram_tensor("r_scratch", (G, P, T, D), F32, kind="Internal").ap()

    ctx = ExitStack()
    with ctx:
        def sb(name, shape, dt=F32):
            return ctx.enter_context(nc.sbuf_tensor(name, shape, dt))

        def sem(name):
            return ctx.enter_context(nc.semaphore(name))

        w1_hi = sb("w1_hi", [P, L, K1, F], F32R)
        w1_lo = sb("w1_lo", [P, L, K1, F], F32R)
        w2_hi = sb("w2_hi", [P, L, C, D], F32R)
        w2_lo = sb("w2_lo", [P, L, C, D], F32R)
        b1_eff = sb("b1_eff", [P, L, C])
        g1_row = sb("g1_row", [P, L, D])
        bb_row = sb("bb_row", [P, L, D])
        g2_row = sb("g2_row", [P, L, D])
        beta2_row = sb("beta2_row", [P, L, D])
        aw_row = sb("aw_row", [P, L, 2 * D])
        ab_col = sb("ab_col", [P, L])
        g1_col = sb("g1_col", [P, L, K1])
        beta1_col = sb("beta1_col", [P, L, K1])
        b1_col = sb("b1_col", [P, L, C])
        a_col = sb("a_col", [O, 2])
        v_row = sb("v_row", [P, 2, D])
        ident = sb("ident", [P, P])
        ident_b = sb("ident_b", [P, P], BF16)
        eye_i = sb("eye_i", [P, P], I32)
        neg_half = sb("neg_half", [P, T])
        spare = sb("spare", [P, 1])

        xb = [sb(f"xb{i}", [P, T, D]) for i in range(2)]
        hb = [sb(f"hb{i}", [P, T, D]) for i in range(2)]
        zt_hi = sb("zt_hi", [P, K1, T * P], F32R)
        zt_lo = sb("zt_lo", [P, K1, T * P], F32R)
        g_hi = sb("g_hi", [P, C, T * P], F32R)
        g_lo = sb("g_lo", [P, C, T * P], F32R)
        e1 = sb("e1", [P, T, P])
        e2 = sb("e2", [P, T, P])
        et = sb("et", [P, T, P])
        wfc = et[0:O, :, :].rearrange("p t m -> p (t m)")[:, 0:D]
        ub = sb("ub", [P, T, D])
        vb = sb("vb", [P, T, D])
        xo = sb("xo", [P, T, D])
        adj_i = sb("adj_i", [P, T, P], I32)
        m1 = [sb(f"m1_{i}", [P, T, P], BF16) for i in range(2)]
        dots = [sb(f"dots_{i}", [P, 2, T]) for i in range(2)]
        junk = sb("junk", [P, 2, D])
        small = sb("small", [P, 5, T])
        cc = sb("cc", [P, 2, T])
        rsum = sb("rsum", [P, T])
        rinv = sb("rinv", [P, T])
        st1 = sb("st1", [P, T, 6])
        mv1 = sb("mv1", [P, T, 2])
        ve1 = sb("ve1", [P, T])
        rs1 = sb("rs1", [P, T])
        st2 = sb("st2", [P, T, 6])
        mv2 = sb("mv2", [P, T, 2])
        ve2 = sb("ve2", [P, T])
        rs2 = sb("rs2", [P, T])

        xin = [sb(f"xin{i}", [P, T, D]) for i in range(2)]
        h0 = [sb(f"h0_{i}", [P, T, D]) for i in range(2)]
        elu_e = vb
        elu_r = sb("elu_r", [P, T, D])
        et0 = sb("et0", [P, T, P])
        m0 = sb("m0", [P, T, P], BF16)
        dots0 = sb("dots0", [P, 2, T])
        small0 = sb("small0", [P, 5, T])
        cc0 = sb("cc0", [P, 2, T])
        rsum0 = sb("rsum0", [P, T])
        rinv0 = sb("rinv0", [P, T])
        st3 = sb("st3", [P, T, 6])
        mv3 = sb("mv3", [P, T, 2])
        ve3 = sb("ve3", [P, T])
        rs3 = sb("rs3", [P, T])
        nm3 = sb("nm3", [P, T])
        st4 = sb("st4", [P, T, 6])
        mv4 = sb("mv4", [P, T, 2])
        ve4 = sb("ve4", [P, T])
        rs4 = sb("rs4", [P, T])
        nm4 = sb("nm4", [P, T])

        bank = [ctx.enter_context(nc.psum_tensor(f"bank{i}", [P, 512], F32)) for i in range(5)]
        ps_y = bank[3:5]
        ps_s = ctx.enter_context(nc.psum_tensor("ps_s", [P, T * P], F32))
        ps_u = [ctx.enter_context(nc.psum_tensor(f"ps_u{i}", [P, 512], F32)) for i in range(2)]

        const_in = sem("const_in")
        w_in = sem("w_in")
        zeroed = sem("zeroed")
        ident_ready = sem("ident_ready")
        b1_ps = sem("b1_ps")
        v_ps = sem("v_ps")
        pro = sem("pro")
        w_ready = sem("w_ready")

        adj_in = sem("adj_in")
        x_in = sem("x_in")
        y_out = sem("y_out")
        r_in = sem("r_in")
        xin_in = sem("xin_in")
        r_out = sem("r_out")

        masks_sum = sem("masks_sum")
        masks_ready = sem("masks_ready")
        dots_ready = sem("dots_ready")
        scores_ready = sem("scores_ready")
        max_steps = sem("max_steps")
        cc_ready = sem("cc_ready")
        e12_ready = sem("e12_ready")
        e_ready = sem("e_ready")
        rinv_ready = sem("rinv_ready")
        et_ps = sem("et_ps")
        et_ready = sem("et_ready")
        agg_done = sem("agg_done")
        u_done = sem("u_done")
        st1_ready = sem("st1_ready")
        mv1_ready = sem("mv1_ready")
        ve1_ready = sem("ve1_ready")
        rs1_ready = sem("rs1_ready")
        z_ready = sem("z_ready")
        h_scaled = sem("h_scaled")
        h_ready = sem("h_ready")
        zt_ps = sem("zt_ps")
        zt_hi_ready = sem("zt_hi_ready")
        zt_lo_ready = sem("zt_lo_ready")
        ff1_done = sem("ff1_done")
        g_hi_ready = sem("g_hi_ready")
        gelu_done = sem("gelu_done")
        g_lo_ready = sem("g_lo_ready")
        ff2_done = sem("ff2_done")
        v_done = sem("v_done")
        st2_ready = sem("st2_ready")
        mv2_ready = sem("mv2_ready")
        ve2_ready = sem("ve2_ready")
        rs2_ready = sem("rs2_ready")
        z2_ready = sem("z2_ready")
        xo_scaled = sem("xo_scaled")
        xo_shifted = sem("xo_shifted")
        xo_ready = sem("xo_ready")

        masks0_ready = sem("masks0_ready")
        dots0_ready = sem("dots0_ready")
        scores0_ready = sem("scores0_ready")
        max0_steps = sem("max0_steps")
        cc0_ready = sem("cc0_ready")
        e12_0_ready = sem("e12_0_ready")
        e0_ready = sem("e0_ready")
        rinv0_ready = sem("rinv0_ready")
        et0_ps = sem("et0_ps")
        et0_ready = sem("et0_ready")
        agg0_done = sem("agg0_done")
        elu_parts = sem("elu_parts")
        elu_sum = sem("elu_sum")
        x1_ready = sem("x1_ready")
        st3_ready = sem("st3_ready")
        mv3_ready = sem("mv3_ready")
        ve3_ready = sem("ve3_ready")
        rs3_ready = sem("rs3_ready")
        nm3_ready = sem("nm3_ready")
        x_made = sem("x_made")
        st4_ready = sem("st4_ready")
        mv4_ready = sem("mv4_ready")
        ve4_ready = sem("ve4_ready")
        rs4_ready = sem("rs4_ready")
        nm4_ready = sem("nm4_ready")
        h0_ready = sem("h0_ready")

        def live(u):
            return 0 <= u < U

        def first(u):
            return 0 <= u < G

        def pick(units, st, u):
            if isinstance(st.off, int):
                return units[u + st.off]
            return units[bass.ds(st.off + u, 1)].rearrange("o n t d -> (o n) t d")

        def steps(eng, body):
            s = -5
            while s <= U:
                if s not in [2] + [l * G + 1 for l in range(1, L)]:
                    body(Step(s))
                    s += 1
                    continue
                n = (G - 5 - s % G) // 2
                with eng.Fori(0, n) as i:
                    i = nc.s_assert_within(i, 0, n - 1, skip_runtime_bounds_check_because="the loop ends before n")
                    for j in range(2):
                        body(Step(s + j, i * 2))
                s += 2 * n

        block = ctx.enter_context(nc.Block())

        @block.sync
        def _(sp):
            def spread(v):
                return v.partition_broadcast(P)

            sp.dma_start(a_col[:, :], w_attn0.rearrange("o (h k) -> k (o h)", h=2),
                         allow_slow_non_contiguous=True).then_inc(const_in, 16)
            sp.dma_start(wfc, w_fc).then_inc(const_in, 16)
            sp.dma_start(beta1_col[:, :, :], beta1.rearrange("l (k p) -> p l k", p=P),
                         allow_slow_non_contiguous=True).then_inc(const_in, 16)
            sp.dma_start(g1_col[:, :, :], g1.rearrange("l (k p) -> p l k", p=P),
                         allow_slow_non_contiguous=True).then_inc(const_in, 16)
            sp.dma_start(b1_col[:, :, :], b1.rearrange("l (c p) -> p l c", p=P),
                         allow_slow_non_contiguous=True).then_inc(const_in, 16)
            sp.dma_start(g1_row[:, :, :], spread(g1)).then_inc(const_in, 16)
            sp.dma_start(bb_row[:, :, :], spread(beta1)).then_inc(const_in, 16)
            sp.dma_start(ub[:, 0:L, :], spread(b2)).then_inc(const_in, 16)
            sp.dma_start(g2_row[:, :, :], spread(g2)).then_inc(const_in, 16)
            sp.dma_start(beta2_row[:, :, :], spread(beta2)).then_inc(const_in, 16)
            sp.dma_start(aw_row[:, :, :], spread(attn_w)).then_inc(const_in, 16)
            sp.dma_start(ab_col[:, :], spread(attn_b)).then_inc(const_in, 16)
            for l in range(L):
                if l:
                    sp.wait_ge(w_ready, K1 * l)
                for k in range(K1):
                    sp.dma_start(xb[k].rearrange("p t d -> p (t d)"), w1[l, k * P:(k + 1) * P, :]).then_inc(w_in, 16)
                    half = C // 2
                    sp.dma_start(hb[k][:, :, :], w2[l].rearrange("(c p) d -> p c d", p=P)[
                        :, k * half:(k + 1) * half, :]).then_inc(w_in, 16)

            def body(st):
                s = st.s
                if live(s + 5):
                    if live(s + 4):
                        sp.wait_ge(masks_ready, st.nth(s + 4))
                    sp.dma_start(adj_i[:, :, :], pick(adj_u, st, (s + 5) % G)).then_inc(adj_in, 16)
                if first(s + 5):
                    if first(s + 3):
                        sp.wait_ge(x1_ready, st.nth(s + 3))
                    elif first(s + 4):
                        sp.wait_ge(st4_ready, st.nth(s + 4))
                    sp.dma_start(xin[(s + 5) % 2][:, :, :], pick(x_u, st, s + 5)).then_inc(xin_in, 16)
                if first(s + 3):
                    sp.wait_ge(x1_ready, st.nth(s + 3))
                    sp.dma_start(pick(r_u, st, s + 3), elu_r[:, :, :]).then_inc(r_out, 16)
                if live(s + 3) and s + 3 >= G:
                    sp.wait_ge(u_done, st.nth(s + 1))
                    sp.dma_start(xb[(s + 3) % 2][:, :, :], pick(y_u, st, s + 3 - G)).then_inc(x_in, 16)
                if live(s - 1):
                    sp.wait_ge(xo_ready, st.nth(s - 1))
                    dst = pick(out_u, st, s - 1 - (L - 1) * G) if s - 1 >= (L - 1) * G else pick(y_u, st, s - 1)
                    sp.dma_start(dst, xo[:, :, :]).then_inc(y_out, 16)
                if live(s) and s >= (L - 1) * G:
                    if s == (L - 1) * G:
                        sp.wait_ge(r_out, 16 * G)
                    sp.dma_start(xin[0][:, :, :], pick(r_u, st, s - (L - 1) * G)).then_inc(r_in, 16)

            steps(sp, body)
            sp.wait_ge(y_out, 16 * U)
            sp.wait_ge(r_out, 16 * G)

        @block.tensor
        def _(pe):
            pe.wait_ge(const_in, 16 * 12)
            for j in range(2):
                mm = pe.matmul(ps_s[:, j * D:(j + 1) * D], a_col[:, j:j + 1].to_broadcast((O, P)), wfc,
                               start=True, stop=True)
            mm.then_inc(v_ps, 1)
            for l in range(L):
                pe.wait_ge(w_in, 16 * 4 * (l + 1))
                if l:
                    pe.wait_ge(w_ready, K1 * l)
                for c in range(C):
                    for k in range(K1):
                        mm = pe.matmul(ps_u[0][:, c:c + 1],
                                       xb[k].rearrange("p t d -> p (t d)")[:, c * P:(c + 1) * P],
                                       beta1_col[:, l, k:k + 1], start=(k == 0), stop=(k == K1 - 1))
                mm.then_inc(b1_ps, 1)
            pe.wait_ge(w_ready, K1 * L)
            pe.wait_ge(ident_ready, 2)

            def score_rows(mask, dot, done):
                for t in range(T):
                    pe.matmul(ps_s[:, t * P:(t + 1) * P], dot[:, 1, t:t + 1].to_broadcast((P, P)), ident[:, :],
                              is_transpose=True, start=(t == 0), stop=True, skip_group_check=True)
                pe.matmul(ps_s[:, :], ident_b[:, :], mask.rearrange("p t m -> p (t m)"),
                          start=False, stop=True, skip_group_check=True).then_inc(done, 1)

            def turn_weights(done):
                for t in range(T):
                    mm = pe.transpose(ps_s[:, t * P:(t + 1) * P], e1[:, t, :], ident[:, :])
                mm.then_inc(done, 1)

            def aggregate(weights, rows, done):
                for t in range(T):
                    pe.matmul(ps_u[t // 2][:, t % 2 * D:(t % 2 + 1) * D], weights[:, t, :], rows[:, t, :],
                              start=True, stop=True).then_inc(done, 1)

            def body(st):
                s = st.s
                l = s // G

                def hidden(c):
                    if not live(s):
                        return
                    if c == 0:
                        pe.wait_ge(zt_hi_ready, st.nth(s))
                        pe.wait_ge(zt_lo_ready, st.nth(s))
                    if c in (3, 4) and live(s - 1):
                        pe.wait_ge(v_done, st.nth(s - 1, 2, c - 2))
                    if c >= 5:
                        pe.wait_ge(g_lo_ready, st.nth(s, C, c - 4))
                    n = 0
                    for k in range(K1):
                        for w, z in ((w1_hi, zt_hi), (w1_hi, zt_lo), (w1_lo, zt_hi)):
                            mm = pe.matmul(bank[c % 5][:, :], w[:, l, k, c * P:(c + 1) * P], z[:, k, :],
                                           start=(n == 0), stop=(n == 3 * K1 - 1))
                            n += 1
                    mm.then_inc(ff1_done, 1)

                def second(r):
                    if not live(s):
                        return
                    for c in range(C):
                        if r == 0:
                            pe.wait_ge(g_lo_ready, st.nth(s, C, max(c + 1, 4)))
                        if r == 2 and c == 0:
                            pe.wait_ge(g_lo_ready, st.nth(s, C))
                        y = ps_y[r // 2][:, r % 2 * D:(r % 2 + 1) * D]
                        for n, (g, w) in enumerate(((g_hi, w2_hi), (g_hi, w2_lo), (g_lo, w2_hi))):
                            mm = pe.matmul(y, g[:, c, r * P:(r + 1) * P], w[:, l, c, :],
                                           start=(c == 0 and n == 0), stop=(c == C - 1 and n == 2))
                    mm.then_inc(ff2_done, 1)

                def transpose_z():
                    if not live(s + 1):
                        return
                    pe.wait_ge(z_ready, st.nth(s + 1))
                    if first(s + 3):
                        pe.wait_ge(elu_parts, st.nth(s + 3))
                    for k in range(K1):
                        for t in range(T):
                            mm = pe.transpose(ps_u[k][:, t * P:(t + 1) * P], ub[:, t, k * P:(k + 1) * P], ident[:, :])
                    mm.then_inc(zt_ps, 1)

                if first(s + 3):
                    pe.wait_ge(e0_ready, st.nth(s + 3))
                    turn_weights(et0_ps)
                hidden(0)
                hidden(1)
                if live(s + 2):
                    pe.wait_ge(dots_ready, st.nth(s + 2, 2 * T))
                    pe.wait_ge(masks_ready, st.nth(s + 2))
                    if first(s + 3):
                        pe.wait_ge(et0_ready, st.nth(s + 3))
                    elif live(s + 1):
                        pe.wait_ge(et_ready, st.nth(s + 1))
                    score_rows(m1[s % 2][:, :, :], dots[s % 2], scores_ready)
                hidden(2)
                if live(s + 1):
                    pe.wait_ge(et_ready, st.nth(s + 1))
                    if live(s):
                        pe.wait_ge(zt_lo_ready, st.nth(s))
                    aggregate(et, xb[(s + 1) % 2], agg_done)
                hidden(3)
                hidden(4)
                hidden(5)
                if first(s + 3):
                    pe.wait_ge(et0_ready, st.nth(s + 3))
                    if live(s + 1):
                        pe.wait_ge(u_done, st.nth(s + 1))
                    aggregate(et0, h0[(s + 3) % 2], agg0_done)
                hidden(6)
                hidden(7)
                second(0)
                if not first(s + 3):
                    transpose_z()
                second(1)
                if live(s + 2):
                    pe.wait_ge(e_ready, st.nth(s + 2))
                    turn_weights(et_ps)
                second(2)
                if first(s + 3):
                    transpose_z()
                second(3)
                if first(s + 4):
                    pe.wait_ge(dots0_ready, st.nth(s + 4, 2 * T))
                    pe.wait_ge(masks0_ready, st.nth(s + 4))
                    if live(s + 2):
                        pe.wait_ge(et_ready, st.nth(s + 2))
                    elif first(s + 3):
                        pe.wait_ge(et0_ready, st.nth(s + 3))
                    score_rows(m0[:, :, :], dots0, scores0_ready)

            steps(pe, body)

        @block.scalar
        def _(act):
            act.wait_ge(w_ready, K1 * L)

            def exps(cols):
                for t in range(T):
                    src = ps_s[:, t * P:(t + 1) * P]
                    act.activation(e1[:, t, :], src, ACT.Exp, bias=cols[:, 0, t:t + 1])
                    a = act.activation(e2[:, t, :], src, ACT.Exp, bias=cols[:, 1, t:t + 1], scale=SLOPE)
                return a

            def norm_relu(dst, src, rs, nm):
                for t in range(T):
                    a = act.activation(dst[:, t, :], src[:, t, :], ACT.Relu, bias=nm[:, t:t + 1], scale=rs[:, t:t + 1])
                return a

            def body(st):
                s = st.s
                if first(s + 3):
                    act.wait_ge(et0_ps, st.nth(s + 3))
                    if first(s + 2):
                        act.wait_ge(agg0_done, st.nth(s + 2, T))
                    act.activation(et0.rearrange("p t m -> p (t m)"), ps_s[:, :], ACT.Copy).then_inc(et0_ready, 1)
                if live(s):
                    for c in range(C):
                        act.wait_ge(ff1_done, st.nth(s, C, c + 1))
                        bias = b1_eff[:, s // G, c:c + 1]
                        act.activation(g_hi[:, c, :], bank[c % 5][:, :], ACT.Gelu, bias=bias).then_inc(g_hi_ready, 1)
                        act.wait_ge(g_hi_ready, st.nth(s, C, c + 1))
                        act.activation(bank[c % 5][:, :], bank[c % 5][:, :], ACT.Gelu, bias=bias).then_inc(gelu_done, 1)
                if live(s + 2):
                    act.wait_ge(cc_ready, st.nth(s + 2))
                    exps(cc).then_inc(e12_ready, 1)
                if first(s + 3):
                    act.wait_ge(rinv0_ready, st.nth(s + 3))
                    if first(s + 2):
                        act.wait_ge(x1_ready, st.nth(s + 2))
                        act.wait_ge(r_out, 16 * st.nth(s + 2))
                        act.wait_ge(x_made, st.nth(s + 2))
                    if live(s - 1):
                        act.wait_ge(xo_scaled, st.nth(s - 1))
                    for t in range(T):
                        if t % 2 == 0:
                            act.wait_ge(agg0_done, st.nth(s + 3, T, t + 2))
                        src = ps_u[t // 2][:, t % 2 * D:(t % 2 + 1) * D]
                        act.activation(elu_e[:, t, :], src, ACT.Exp, scale=rinv0[:, t:t + 1])
                        a = act.activation(elu_r[:, t, :], src, ACT.Relu, scale=rinv0[:, t:t + 1])
                    a.then_inc(elu_parts, 1)
                if live(s + 1) and not first(s + 3):
                    transposed_high(st)
                if live(s + 2):
                    act.wait_ge(et_ps, st.nth(s + 2))
                    if live(s + 1):
                        act.wait_ge(agg_done, st.nth(s + 1, T))
                    act.activation(et.rearrange("p t m -> p (t m)"), ps_s[:, :], ACT.Copy).then_inc(et_ready, 1)
                if live(s + 1) and first(s + 3):
                    transposed_high(st)
                if first(s + 3):
                    act.wait_ge(nm3_ready, st.nth(s + 3))
                    if live(s + 1):
                        act.wait_ge(u_done, st.nth(s + 1))
                        act.wait_ge(agg_done, st.nth(s + 1, T))
                    norm_relu(xb[(s + 3) % 2], elu_r, rs3, nm3).then_inc(x_made, 1)
                if first(s + 4):
                    act.wait_ge(cc0_ready, st.nth(s + 4))
                    if live(s + 2):
                        act.wait_ge(et_ps, st.nth(s + 2))
                    exps(cc0).then_inc(e12_0_ready, 1)
                if first(s + 5):
                    act.wait_ge(nm4_ready, st.nth(s + 5))
                    if first(s + 3):
                        act.wait_ge(agg0_done, st.nth(s + 3, T))
                    norm_relu(h0[(s + 5) % 2], xin[(s + 5) % 2], rs4, nm4).then_inc(h0_ready, 1)

            def transposed_high(st):
                act.wait_ge(zt_ps, st.nth(st.s + 1))
                for k in range(K1):
                    a = act.activation(zt_hi[:, k, :], ps_u[k][:, :], ACT.Copy)
                a.then_inc(zt_hi_ready, 1)

            steps(act, body)

        @block.vector
        def _(dve):
            done = [0]

            def link(ins):
                done[0] += 1
                ins.then_inc(pro, 1)
                dve.wait_ge(pro, done[0])

            link(dve.memset(neg_half[:, :], -0.5))
            dve.wait_ge(const_in, 16 * 12)
            link(dve.tensor_tensor(bb_row[:, :, :], bb_row[:, :, :], ub[:, 0:L, :], ALU.add))
            dve.wait_ge(v_ps, 1)
            link(dve.tensor_copy(v_row.rearrange("p a d -> p (a d)"), ps_s[:, :]))
            for l in range(L):
                dve.wait_ge(w_in, 16 * 4 * (l + 1))
                dve.wait_ge(b1_ps, l + 1)
                link(dve.tensor_tensor(b1_eff[:, l, :], ps_u[0][:, 0:C], b1_col[:, l, :], ALU.add))
                half = C // 2
                for k in range(K1):
                    raw = xb[k].rearrange("p t d -> p (t d)")
                    link(dve.tensor_scalar(raw, raw, g1_col[:, l, k:k + 1], None, ALU.mult))
                    dve.tensor_copy(w1_hi[:, l, k, :], raw)
                    link(dve.tensor_copy(w2_hi[:, l, k * half:(k + 1) * half, :], hb[k][:, :, :]))
                    link(dve.tensor_tensor(w1_lo[:, l, k, :], raw, w1_hi[:, l, k, :].bitcast(F32), ALU.subtract))
                    dve.tensor_tensor(w2_lo[:, l, k * half:(k + 1) * half, :], hb[k][:, :, :],
                                      w2_hi[:, l, k * half:(k + 1) * half, :].bitcast(F32),
                                      ALU.subtract).then_inc(w_ready, 1)

            def branch_biases(st, u, sm, dot, cols, per_head, steps_sem, ready):
                dve.tensor_reduce(sm[:, 0, :], ps_s.rearrange("p (t m) -> p t m", t=T), AX, ALU.max)
                if per_head is None:
                    dve.tensor_copy(sm[:, 1, :], dot[:, 0, :]).then_inc(steps_sem, 1)
                else:
                    dve.tensor_scalar(sm[:, 1, :], dot[:, 0, :], per_head, None, ALU.add).then_inc(steps_sem, 1)
                dve.wait_ge(steps_sem, st.nth(u, 3, 1))
                dve.tensor_tensor(sm[:, 2, :], sm[:, 0, :], sm[:, 1, :], ALU.add).then_inc(steps_sem, 1)
                dve.wait_ge(steps_sem, st.nth(u, 3, 2))
                dve.scalar_tensor_tensor(out=sm[:, 3, :], in0=sm[:, 2, :], scalar=SLOPE, in1=sm[:, 2, :],
                                         op0=ALU.mult, op1=ALU.max).then_inc(steps_sem, 1)
                dve.wait_ge(steps_sem, st.nth(u, 3, 3))
                dve.tensor_tensor(cols[:, 0, :], sm[:, 1, :], sm[:, 3, :], ALU.subtract)
                dve.scalar_tensor_tensor(out=cols[:, 1, :], in0=sm[:, 1, :], scalar=SLOPE, in1=sm[:, 3, :],
                                         op0=ALU.mult, op1=ALU.subtract).then_inc(ready, 1)

            def weights(st, u, rs, ri, e12, e_done, r_done):
                dve.wait_ge(e12, st.nth(u))
                for t in range(T):
                    ins = dve.scalar_tensor_tensor(out=e1[:, t, :], in0=e1[:, t, :], scalar=1.0, in1=e2[:, t, :],
                                                   op0=ALU.mult, op1=ALU.max, accum_out=rs[:, t:t + 1])
                ins.then_inc(e_done, 1)
                dve.wait_ge(e_done, st.nth(u))
                dve.reciprocal(ri[:, :], rs[:, :]).then_inc(r_done, 1)

            def row_dots(st, u, dot, rows, vec, ready):
                for t in range(T):
                    for j in range(2):
                        if t:
                            dve.wait_ge(ready, st.nth(u, 2 * T, 2 * t + j - 1))
                        dve.tensor_tensor_reduce(junk[:, j, :], rows[:, t, :], vec(j), 1.0, 0.0,
                                                 ALU.mult, ALU.add, dot[:, j, t:t + 1]).then_inc(ready, 1)

            def statistics(rows, st_t, ready):
                for t in range(T):
                    ins = dve.bn_stats(st_t[:, t, :], rows[:, t, :])
                ins.then_inc(ready, 1)

            def variance(st, u, st_t, mv, ve, mv_ready, ve_ready):
                for t in range(T):
                    ins = dve.bn_aggr(mv[:, t, :], st_t[:, t, :])
                ins.then_inc(mv_ready, 1)
                dve.wait_ge(mv_ready, st.nth(u))
                dve.tensor_scalar(ve[:, :], mv[:, :, 1], EPS, None, ALU.add).then_inc(ve_ready, 1)

            def normalise(rows, mv, rs, ready):
                for t in range(T):
                    ins = dve.tensor_scalar(rows[:, t, :], rows[:, t, :], mv[:, t, 0:1], rs[:, t:t + 1],
                                            ALU.subtract, ALU.mult)
                ins.then_inc(ready, 1)

            def body(st):
                s = st.s

                def g_low(c):
                    if not live(s):
                        return
                    dve.wait_ge(gelu_done, st.nth(s, C, c + 1))
                    dve.tensor_tensor(g_lo[:, c, :], bank[c % 5][:, :], g_hi[:, c, :].bitcast(F32),
                                      ALU.subtract).then_inc(g_lo_ready, 1)

                if live(s - 1):
                    dve.wait_ge(h_ready, st.nth(s - 1))
                    if live(s - 2):
                        dve.wait_ge(xo_scaled, st.nth(s - 2))
                    for r in range(2):
                        dve.wait_ge(ff2_done, st.nth(s - 1, T, 2 * r + 2))
                        dve.tensor_tensor(vb[:, 2 * r:2 * r + 2, :], ps_y[r].rearrange("p (t d) -> p t d", d=D),
                                          hb[(s - 1) % 2][:, 2 * r:2 * r + 2, :], ALU.add).then_inc(v_done, 1)
                    dve.wait_ge(v_done, st.nth(s - 1, 2))
                    statistics(vb, st2, st2_ready)
                    dve.wait_ge(st2_ready, st.nth(s - 1))
                g_low(0)
                if live(s - 1):
                    variance(st, s - 1, st2, mv2, ve2, mv2_ready, ve2_ready)
                g_low(1)
                if live(s + 2):
                    dve.wait_ge(scores_ready, st.nth(s + 2))
                    if live(s + 1):
                        dve.wait_ge(e12_ready, st.nth(s + 1))
                    branch_biases(st, s + 2, small, dots[s % 2], cc, ab_col[:, (s + 2) // G:(s + 2) // G + 1],
                                  max_steps, cc_ready)
                g_low(2)
                if live(s - 1):
                    dve.wait_ge(rs2_ready, st.nth(s - 1))
                    normalise(vb, mv2, rs2, z2_ready)
                g_low(3)
                for half in range(2):
                    if live(s + 1):
                        if half == 0 and live(s):
                            dve.wait_ge(h_ready, st.nth(s))
                            dve.wait_ge(zt_ps, st.nth(s))
                        dve.wait_ge(agg_done, st.nth(s + 1, T, 2 * half + 2))
                        for t in range(2 * half, 2 * half + 2):
                            ins = dve.scalar_tensor_tensor(
                                out=ub[:, t, :], in0=ps_u[t // 2][:, t % 2 * D:(t % 2 + 1) * D],
                                scalar=rinv[:, t:t + 1], in1=xb[(s + 1) % 2][:, t, :], op0=ALU.mult, op1=ALU.add)
                        if half:
                            ins.then_inc(u_done, 1)
                    g_low(4 + half)
                if live(s + 1):
                    dve.wait_ge(u_done, st.nth(s + 1))
                    statistics(ub, st1, st1_ready)
                    dve.wait_ge(st1_ready, st.nth(s + 1))
                g_low(6)
                if live(s + 1):
                    variance(st, s + 1, st1, mv1, ve1, mv1_ready, ve1_ready)
                g_low(7)
                if live(s + 1):
                    dve.wait_ge(rs1_ready, st.nth(s + 1))
                    normalise(ub, mv1, rs1, z_ready)
                if live(s + 2):
                    weights(st, s + 2, rsum, rinv, e12_ready, e_ready, rinv_ready)
                if first(s + 3):
                    dve.wait_ge(elu_parts, st.nth(s + 3))
                    dve.scalar_tensor_tensor(out=elu_e.rearrange("p t d -> p (t d)"),
                                             in0=elu_e.rearrange("p t d -> p (t d)"), scalar=1.0,
                                             in1=elu_r.rearrange("p t d -> p (t d)"),
                                             op0=ALU.min, op1=ALU.add).then_inc(elu_sum, 1)
                    dve.wait_ge(elu_sum, st.nth(s + 3))
                    dve.scalar_tensor_tensor(out=elu_r.rearrange("p t d -> p (t d)"),
                                             in0=elu_e.rearrange("p t d -> p (t d)"), scalar=-1.0,
                                             in1=xin[(s + 3) % 2].rearrange("p t d -> p (t d)"),
                                             op0=ALU.add, op1=ALU.add).then_inc(x1_ready, 1)
                    dve.wait_ge(x1_ready, st.nth(s + 3))
                    statistics(elu_r, st3, st3_ready)
                    dve.wait_ge(st3_ready, st.nth(s + 3))
                if live(s + 1):
                    dve.wait_ge(zt_hi_ready, st.nth(s + 1))
                    for k in range(K1):
                        ins = dve.tensor_tensor(zt_lo[:, k, :], ps_u[k][:, :], zt_hi[:, k, :].bitcast(F32),
                                                ALU.subtract)
                    ins.then_inc(zt_lo_ready, 1)
                if first(s + 3):
                    variance(st, s + 3, st3, mv3, ve3, mv3_ready, ve3_ready)
                if first(s + 5):
                    dve.wait_ge(xin_in, 16 * st.nth(s + 5))
                    statistics(xin[(s + 5) % 2], st4, st4_ready)
                    dve.wait_ge(st4_ready, st.nth(s + 5))
                if first(s + 3):
                    dve.wait_ge(rs3_ready, st.nth(s + 3))
                    dve.scalar_tensor_tensor(out=nm3[:, :], in0=mv3[:, :, 0], scalar=-1.0, in1=rs3[:, :],
                                             op0=ALU.mult, op1=ALU.mult).then_inc(nm3_ready, 1)
                if first(s + 5):
                    variance(st, s + 5, st4, mv4, ve4, mv4_ready, ve4_ready)
                if first(s + 4):
                    dve.wait_ge(scores0_ready, st.nth(s + 4))
                    branch_biases(st, s + 4, small0, dots0, cc0, None, max0_steps, cc0_ready)
                if first(s + 5):
                    dve.wait_ge(rs4_ready, st.nth(s + 5))
                    dve.scalar_tensor_tensor(out=nm4[:, :], in0=mv4[:, :, 0], scalar=-1.0, in1=rs4[:, :],
                                             op0=ALU.mult, op1=ALU.mult).then_inc(nm4_ready, 1)
                if live(s + 3):
                    if s + 3 < G:
                        dve.wait_ge(x_made, st.nth(s + 3))
                    else:
                        dve.wait_ge(x_in, 16 * st.nth(s + 3 - G))
                    l3 = (s + 3) // G
                    row_dots(st, s + 3, dots[(s + 3) % 2], xb[(s + 3) % 2],
                             lambda j: aw_row[:, l3, j * D:(j + 1) * D], dots_ready)
                if first(s + 4):
                    weights(st, s + 4, rsum0, rinv0, e12_0_ready, e0_ready, rinv0_ready)
                if first(s + 5):
                    dve.wait_ge(h0_ready, st.nth(s + 5))
                    row_dots(st, s + 5, dots0, h0[(s + 5) % 2], lambda j: v_row[:, j, :], dots0_ready)

            steps(dve, body)

        @block.gpsimd
        def _(pool):
            pool.memset(ident[:, :], 0.0).then_inc(zeroed, 1)
            pool.memset(ident_b[:, :], 0.0).then_inc(zeroed, 1)
            pool.wait_ge(zeroed, 2)
            for m in (ident, ident_b):
                pool.affine_select(out=m[:, :], in_=m[:, :], compare_op=ALU.not_equal, fill=1.0, base=0,
                                   pattern=[[-1, P]], channel_multiplier=1).then_inc(ident_ready, 1)
            pool.wait_ge(ident_ready, 2)
            pool.tensor_copy(eye_i[:, :], ident[:, :]).then_inc(ident_ready, 1)
            pool.wait_ge(ident_ready, 3)
            pool.wait_ge(w_ready, K1 * L)

            def all_graphs(row):
                return row.unsqueeze(1).to_broadcast((P, T, D))

            def take_waits():
                pool.tensor_tensor(spare[:, :], neg_half[:, 0:1], neg_half[:, 0:1], ALU.mult)

            def inverse_root(u, st, ve, rs, ve_ready, rs_ready):
                pool.wait_ge(ve_ready, st.nth(u))
                pool.tensor_tensor(rs[:, :], ve[:, :], neg_half[:, :], ALU.pow).then_inc(rs_ready, 1)

            def body(st):
                s = st.s
                if live(s - 1):
                    inverse_root(s - 1, st, ve2, rs2, ve2_ready, rs2_ready)
                if live(s + 4):
                    pool.wait_ge(adj_in, 16 * st.nth(s + 4))
                    if first(s + 4):
                        if first(s + 3):
                            pool.wait_ge(scores0_ready, st.nth(s + 3))
                        take_waits()
                        pool.tensor_scalar(m0[:, :, :], adj_i[:, :, :], 0.0, -BIG,
                                           ALU.is_equal, ALU.mult).then_inc(masks0_ready, 1)
                        pool.wait_ge(masks0_ready, st.nth(s + 4))
                    pool.tensor_tensor(adj_i[:, :, :], adj_i[:, :, :], eye_i[:, :].unsqueeze(1).to_broadcast((P, T, P)),
                                       ALU.add).then_inc(masks_sum, 1)
                    pool.wait_ge(masks_sum, st.nth(s + 4))
                    if live(s + 2):
                        pool.wait_ge(scores_ready, st.nth(s + 2))
                    take_waits()
                    pool.tensor_scalar(m1[s % 2][:, :, :], adj_i[:, :, :], 0.0, -BIG,
                                       ALU.is_le, ALU.mult).then_inc(masks_ready, 1)
                if live(s - 1):
                    l = (s - 1) // G
                    last = l == L - 1
                    pool.wait_ge(z2_ready, st.nth(s - 1))
                    if live(s - 2):
                        pool.wait_ge(y_out, 16 * st.nth(s - 2))
                    pool.tensor_tensor(xo[:, :, :], vb[:, :, :], all_graphs(g2_row[:, l, :]),
                                       ALU.mult).then_inc(xo_scaled, 1)
                    pool.wait_ge(xo_scaled, st.nth(s - 1))
                    pool.tensor_tensor(xo[:, :, :], xo[:, :, :], all_graphs(beta2_row[:, l, :]),
                                       ALU.add).then_inc(xo_shifted if last else xo_ready, 1)
                    if last:
                        nth = st.nth(s - 1 - (L - 1) * G)
                        pool.wait_ge(xo_shifted, nth)
                        pool.wait_ge(r_in, 16 * nth)
                        pool.tensor_tensor(xo[:, :, :], xo[:, :, :], xin[0][:, :, :], ALU.add).then_inc(xo_ready, 1)
                if live(s + 1):
                    l = (s + 1) // G
                    inverse_root(s + 1, st, ve1, rs1, ve1_ready, rs1_ready)
                    pool.wait_ge(z_ready, st.nth(s + 1))
                    if live(s - 1):
                        pool.wait_ge(v_done, st.nth(s - 1, 2))
                    h = hb[(s + 1) % 2]
                    pool.tensor_tensor(h[:, :, :], ub[:, :, :], all_graphs(g1_row[:, l, :]), ALU.mult).then_inc(h_scaled, 1)
                    pool.wait_ge(h_scaled, st.nth(s + 1))
                    pool.tensor_tensor(h[:, :, :], h[:, :, :], all_graphs(bb_row[:, l, :]), ALU.add).then_inc(h_ready, 1)
                if first(s + 3):
                    inverse_root(s + 3, st, ve3, rs3, ve3_ready, rs3_ready)
                if first(s + 5):
                    inverse_root(s + 5, st, ve4, rs4, ve4_ready, rs4_ready)

            steps(pool, body)


_INS = ["x", "adj", "L0_gnn_W_fc", "L0_gnn_W_attn", "L1_gnn_attn_w", "L1_gnn_attn_b", "L1_gnn_W1", "L1_gnn_b1",
        "L1_gnn_W2", "L1_gnn_b2", "L1_gnn_g1", "L1_gnn_beta1", "L1_gnn_g2", "L1_gnn_beta2"]


def kernel(**inputs):
    import numpy as np
    import concourse.bacc as bacc
    from concourse import mybir as mb
    from concourse.bass_utils import run_bass_kernel_spmd

    nc = bacc.Bacc("TRN2", target_bir_lowering=False, num_devices=1, dynamic_dma_scratch_size=1024)
    arrays, args = {}, []
    for name in _INS:
        a = np.ascontiguousarray(inputs[name])
        arrays[f"in_{name}"] = a
        args.append(nc.dram_tensor(f"in_{name}", a.shape, mb.dt.from_np(a.dtype), kind="ExternalInput").ap())
    out = nc.dram_tensor("out", inputs["x"].shape, mb.dt.float32, kind="ExternalOutput").ap()
    build(nc, *args, out)
    r = run_bass_kernel_spmd(nc, [arrays], core_ids=[0])
    return r.results[0]["out"]
```

```python
from contextlib import ExitStack

import concourse.bass as bass
from concourse import mybir

ALU = mybir.AluOpType
ACT = mybir.ActivationFunctionType
AX = mybir.AxisListType.X
F32 = mybir.dt.float32
F32R = mybir.dt.float32r
BF16 = mybir.dt.bfloat16
I32 = mybir.dt.int32

P = 128
T = 4
EPS = 1e-5
SLOPE = 0.2
BIG = 2.0 ** 100


class Step:

    def __init__(self, s, off=0, off0=0):
        self.s, self.off, self.off0 = s, off, off0

    def nth(self, unit, per=1, j=None):
        return unit * per + (per if j is None else j) + self.off * per

    def nth0(self, group, per=1, j=None):
        return group * per + (per if j is None else j) + self.off0 * per


def build(nc, x, adj, w_fc, w_attn0, attn_w, attn_b, w1, b1, w2, b2, g1, beta1, g2, beta2, out):
    B, N, D = x.shape
    L = w1.shape[0]
    F = w1.shape[2]
    O = w_fc.shape[0]
    K1 = D // P
    C = F // P
    G = B // T
    CH = 8
    PER = L * CH
    FILL = 7
    U = L * G
    assert N == P and K1 == 2 and C == 8 and L == 3 and G % CH == 0

    def layer(n):
        return n % PER // CH

    def group(n):
        return n // PER * CH + n % CH

    x_u = x.rearrange("(g t) n d -> g n t d", t=T)
    adj_u = adj.rearrange("(g t) n m -> g n t m", t=T)
    out_u = out.rearrange("(g t) n d -> g n t d", t=T)
    xs_u = nc.dram_tensor("x_scratch", (L * G, P, T, D), F32, kind="Internal").ap()
    r_u = nc.dram_tensor("r_scratch", (G, P, T, D), F32, kind="Internal").ap()
    m_u = nc.dram_tensor("m_scratch", (G, P, T, P // 2), I32, kind="Internal").ap()

    ctx = ExitStack()
    with ctx:
        def sb(name, shape, dt=F32):
            return ctx.enter_context(nc.sbuf_tensor(name, shape, dt))

        def sem(name):
            return ctx.enter_context(nc.semaphore(name))

        w1_hi = sb("w1_hi", [P, L, K1, F], F32R)
        w1_lo = sb("w1_lo", [P, L, K1, F], F32R)
        w2_hi = sb("w2_hi", [P, L, C, D], F32R)
        w2_lo = sb("w2_lo", [P, L, C, D], F32R)
        b1_eff = sb("b1_eff", [P, L, C])
        g1_row = sb("g1_row", [P, L, D])
        bb_row = sb("bb_row", [P, L, D])
        g2_row = sb("g2_row", [P, L, D])
        beta2_row = sb("beta2_row", [P, L, D])
        aw_row = sb("aw_row", [P, L, 2 * D])
        ab_col = sb("ab_col", [P, L])
        g1_col = sb("g1_col", [P, L, K1])
        beta1_col = sb("beta1_col", [P, L, K1])
        b1_col = sb("b1_col", [P, L, C])
        a_col = sb("a_col", [O, 2])
        v_row = sb("v_row", [P, 2, D])
        ident = sb("ident", [P, P])
        ident_b = sb("ident_b", [P, P], BF16)
        eye_i = sb("eye_i", [P, P], I32)
        neg_half = sb("neg_half", [P, T])
        spare = sb("spare", [P, 1])

        xb = [sb(f"xb{i}", [P, T, D]) for i in range(2)]
        hb = [sb(f"hb{i}", [P, T, D]) for i in range(2)]
        zt_hi = sb("zt_hi", [P, K1, T * P], F32R)
        zt_lo = sb("zt_lo", [P, K1, T * P], F32R)
        g_hi = sb("g_hi", [P, C, T * P], F32R)
        g_lo = sb("g_lo", [P, C, T * P], F32R)
        e1 = sb("e1", [P, T, P])
        e2 = sb("e2", [P, T, P])
        et = sb("et", [P, T, P])
        wfc = et[0:O, :, :].rearrange("p t m -> p (t m)")[:, 0:D]
        ub = sb("ub", [P, T, D])
        vb = sb("vb", [P, T, D])
        xo = sb("xo", [P, T, D])
        adj_i = sb("adj_i", [P, T, P], I32)
        g_full = adj_i.rearrange("p t m -> p (t m)").bitcast(F32)
        m1 = [sb(f"m1_{i}", [P, T, P], BF16) for i in range(2)]
        m_new = sb("m_new", [P, T, P], BF16)
        dots = [sb(f"dots_{i}", [P, 2, T]) for i in range(2)]
        junk = ub
        small = sb("small", [P, 5, T])
        cc = sb("cc", [P, 2, T])
        rsum = sb("rsum", [P, T])
        rinv = sb("rinv", [P, T])
        st1 = sb("st1", [P, T, 6])
        mv1 = sb("mv1", [P, T, 2])
        ve1 = sb("ve1", [P, T])
        rs1 = sb("rs1", [P, T])
        st2 = sb("st2", [P, T, 6])
        mv2 = sb("mv2", [P, T, 2])
        ve2 = sb("ve2", [P, T])
        rs2 = sb("rs2", [P, T])

        xin = [sb(f"xin{i}", [P, T, D]) for i in range(2)]
        h0 = [sb(f"h0_{i}", [P, T, D]) for i in range(2)]
        elu_e = vb
        elu_r = sb("elu_r", [P, T, D])
        et0 = sb("et0", [P, T, P])
        m0 = sb("m0", [P, T, P], BF16)
        dots0 = sb("dots0", [P, 2, T])
        small0 = sb("small0", [P, 5, T])
        cc0 = sb("cc0", [P, 2, T])
        rsum0 = sb("rsum0", [P, T])
        rinv0 = sb("rinv0", [P, T])
        st3 = sb("st3", [P, T, 6])
        mv3 = sb("mv3", [P, T, 2])
        ve3 = sb("ve3", [P, T])
        rs3 = sb("rs3", [P, T])
        nm3 = sb("nm3", [P, T])
        st4 = sb("st4", [P, T, 6])
        mv4 = sb("mv4", [P, T, 2])
        ve4 = sb("ve4", [P, T])
        rs4 = sb("rs4", [P, T])
        nm4 = sb("nm4", [P, T])

        HC = C // 2
        raw1 = [xb, [ub, vb]]
        raw2 = [hb, [xo, elu_r]]

        bank = [ctx.enter_context(nc.psum_tensor(f"bank{i}", [P, 512], F32)) for i in range(4)]
        ps_y = bank[2:4]
        turn = [0, 1, 2, 3, 0, 2, 1, 3]
        ps_s = ctx.enter_context(nc.psum_tensor("ps_s", [P, T * P], F32))
        ps_s0 = ctx.enter_context(nc.psum_tensor("ps_s0", [P, T * P], F32))
        ps_u = [ctx.enter_context(nc.psum_tensor(f"ps_u{i}", [P, 512], F32)) for i in range(2)]

        const_in = sem("const_in")
        w_in = [sem(f"w_in{l}") for l in range(L)]
        zeroed = sem("zeroed")
        ident_ready = sem("ident_ready")
        b1_ps = sem("b1_ps")
        v_ps = sem("v_ps")
        pro = sem("pro")
        w_hi_ready = sem("w_hi_ready")
        w_ready = sem("w_ready")
        b1_ready = sem("b1_ready")

        adj_in = sem("adj_in")
        x_in = sem("x_in")
        y_out = sem("y_out")
        r_in = sem("r_in")
        m_in = sem("m_in")
        m_out = sem("m_out")
        h_out = sem("h_out")
        xin_in = sem("xin_in")
        xr_in = sem("xr_in")
        r_out = sem("r_out")

        masks_sum = sem("masks_sum")
        masks_ready = sem("masks_ready")
        dots_ready = sem("dots_ready")
        scores_ready = sem("scores_ready")
        max_steps = sem("max_steps")
        cc_ready = sem("cc_ready")
        e12_ready = sem("e12_ready")
        e_ready = sem("e_ready")
        rinv_ready = sem("rinv_ready")
        et_ps = sem("et_ps")
        et_ready = sem("et_ready")
        agg_done = sem("agg_done")
        u_done = sem("u_done")
        st1_ready = sem("st1_ready")
        mv1_ready = sem("mv1_ready")
        ve1_ready = sem("ve1_ready")
        rs1_ready = sem("rs1_ready")
        z_ready = sem("z_ready")
        h_scaled = sem("h_scaled")
        h_ready = sem("h_ready")
        zt_ps = sem("zt_ps")
        zt_hi_ready = sem("zt_hi_ready")
        zt_lo_ready = sem("zt_lo_ready")
        ff1_done = sem("ff1_done")
        g_hi_ready = sem("g_hi_ready")
        gelu_done = sem("gelu_done")
        g_lo_ready = sem("g_lo_ready")
        g_lo_pool = sem("g_lo_pool")
        ff2_done = sem("ff2_done")
        v_done = sem("v_done")
        st2_ready = sem("st2_ready")
        mv2_ready = sem("mv2_ready")
        ve2_ready = sem("ve2_ready")
        rs2_ready = sem("rs2_ready")
        z2_ready = sem("z2_ready")
        xo_scaled = sem("xo_scaled")
        xo_shifted = sem("xo_shifted")
        xo_ready = sem("xo_ready")

        masks0_ready = sem("masks0_ready")
        dots0_ready = sem("dots0_ready")
        scores0_ready = sem("scores0_ready")
        max0_steps = sem("max0_steps")
        cc0_ready = sem("cc0_ready")
        e12_0_ready = sem("e12_0_ready")
        e0_ready = sem("e0_ready")
        rinv0_ready = sem("rinv0_ready")
        et0_ps = sem("et0_ps")
        et0_ready = sem("et0_ready")
        agg0_done = sem("agg0_done")
        elu_parts = sem("elu_parts")
        elu_sum = sem("elu_sum")
        x1_ready = sem("x1_ready")
        st3_ready = sem("st3_ready")
        mv3_ready = sem("mv3_ready")
        ve3_ready = sem("ve3_ready")
        rs3_ready = sem("rs3_ready")
        nm3_ready = sem("nm3_ready")
        x_made = sem("x_made")
        st4_ready = sem("st4_ready")
        mv4_ready = sem("mv4_ready")
        ve4_ready = sem("ve4_ready")
        rs4_ready = sem("rs4_ready")
        nm4_ready = sem("nm4_ready")
        h0_ready = sem("h0_ready")

        def live(u):
            return 0 <= u < U

        def early_step(v):
            return v - FILL if v < CH else 2 + L * (v - CH)

        stage_of = {early_step(v) + j: {} for v in range(G) for j in range(4)}
        for v in range(G):
            for j in range(4):
                stage_of[early_step(v) + j][j] = v

        def early(s):
            return stage_of.get(s, {}).get(0)

        def middle(s):
            return stage_of.get(s, {}).get(1)

        def late(s):
            return stage_of.get(s, {}).get(2)

        def end(s):
            return stage_of.get(s, {}).get(3)

        def residual_x(v):
            return xin[1] if v < CH else xin[0]

        def made(v):
            return xin[1] if v < CH else h0[v % 2]

        POOL_LOW = (2, 5)

        def low_done(eng, st, s, c):
            own = [b for b in range(c + 1) if b in POOL_LOW]
            eng.wait_ge(g_lo_ready, st.nth(s, C - len(POOL_LOW), c + 1 - len(own)))
            if own:
                eng.wait_ge(g_lo_pool, st.nth(s, len(POOL_LOW), len(own)))

        def pick(units, st, u):
            if isinstance(st.off, int):
                return units[u]
            return units[bass.ds(st.off0 + u, 1)].rearrange("o n t d -> (o n) t d")

        def steps(eng, body):
            for s in range(-FILL, PER):
                body(Step(s))
            n = G // CH - 2
            with eng.Fori(0, n) as i:
                i = nc.s_assert_within(i, 0, n - 1, skip_runtime_bounds_check_because="the loop ends before n")
                for s in range(PER, 2 * PER):
                    body(Step(s, i * PER, i * CH))
            for s in range(U - PER, U + 2):
                body(Step(s))

        block = ctx.enter_context(nc.Block())

        @block.sync
        def _(sp):
            def spread(v):
                return v.partition_broadcast(P)

            sp.dma_start(a_col[:, :], w_attn0.rearrange("o (h k) -> k (o h)", h=2),
                         allow_slow_non_contiguous=True).then_inc(const_in, 16)
            sp.dma_start(wfc, w_fc).then_inc(const_in, 16)
            sp.dma_start(beta1_col[:, :, :], beta1.rearrange("l (k p) -> p l k", p=P),
                         allow_slow_non_contiguous=True).then_inc(const_in, 16)
            sp.dma_start(g1_col[:, :, :], g1.rearrange("l (k p) -> p l k", p=P),
                         allow_slow_non_contiguous=True).then_inc(const_in, 16)
            sp.dma_start(b1_col[:, :, :], b1.rearrange("l (c p) -> p l c", p=P),
                         allow_slow_non_contiguous=True).then_inc(const_in, 16)
            sp.dma_start(g1_row[:, :, :], spread(g1)).then_inc(const_in, 16)
            sp.dma_start(bb_row[:, :, :], spread(beta1)).then_inc(const_in, 16)
            sp.dma_start(h0[0][:, 0:L, :], spread(b2)).then_inc(const_in, 16)
            sp.dma_start(g2_row[:, :, :], spread(g2)).then_inc(const_in, 16)
            sp.dma_start(beta2_row[:, :, :], spread(beta2)).then_inc(const_in, 16)
            sp.dma_start(aw_row[:, :, :], spread(attn_w)).then_inc(const_in, 16)
            sp.dma_start(ab_col[:, :], spread(attn_b)).then_inc(const_in, 16)
            for l in range(L):
                if l >= 2:
                    sp.wait_ge(w_hi_ready, 2 * K1 * (l - 1))
                    sp.wait_ge(w_ready, 2 * K1 * (l - 1))
                    sp.wait_ge(b1_ps, l - 1)
                for k in range(K1):
                    sp.dma_start(raw1[l % 2][k].rearrange("p t d -> p (t d)"),
                                 w1[l, k * P:(k + 1) * P, :]).then_inc(w_in[l], 16)
                    sp.dma_start(raw2[l % 2][k][:, :, :], w2[l].rearrange("(c p) d -> p c d", p=P)[
                        :, k * HC:(k + 1) * HC, :]).then_inc(w_in[l], 16)
            sp.wait_ge(w_hi_ready, 2 * K1 * L)

            def body(st):
                s = st.s
                v0, v2, v3 = early(s), late(s), end(s)
                if v0 is not None:
                    if v0 > CH:
                        sp.wait_ge(x1_ready, st.nth0(v0 - 1))
                    elif v0:
                        sp.wait_ge(h0_ready, st.nth0(v0 - 1))
                    sp.dma_start(xin[0][:, :, :], pick(x_u, st, v0)).then_inc(xin_in, 16)
                if live(s + 3):
                    if live(s + 2):
                        sp.wait_ge(scores_ready, st.nth(s + 2))
                    sp.dma_start(m1[(s + 3) % 2][:, :, :].bitcast(I32), pick(m_u, st, group(s + 3))).then_inc(m_in, 16)
                    if layer(s + 3) == 0 and (group(s + 3) < CH or group(s + 3) == G - 1):
                        sp.wait_ge(h_out, 16 * st.nth0(group(s + 3)))
                    if live(s + 1):
                        sp.wait_ge(u_done, st.nth(s + 1))
                    sp.dma_start(xb[(s + 3) % 2][:, :, :],
                                 pick(xs_u, st, layer(s + 3) * G + group(s + 3))).then_inc(x_in, 16)
                if live(s - 2):
                    if s >= PER and live(s + 4) and layer(s + 4) == 0 and group(s + 4) % CH == CH - 1:
                        sp.wait_ge(h_out, 16 * st.nth0(group(s + 4)))
                    sp.wait_ge(xo_ready, st.nth(s - 2))
                    l, g = layer(s - 2), group(s - 2)
                    dst = pick(out_u, st, g) if l == L - 1 else pick(xs_u, st, (l + 1) * G + g)
                    sp.dma_start(dst, xo[:, :, :]).then_inc(y_out, 16)
                if live(s - 1) and layer(s - 1) == L - 1:
                    sp.dma_start(xin[1][:, :, :], pick(r_u, st, group(s - 1))).then_inc(r_in, 16)
                if v0 is not None:
                    if live(s):
                        sp.wait_ge(g_lo_pool, st.nth(s, 2))
                    if v0:
                        sp.wait_ge(masks_ready, st.nth0(v0 - 1))
                    sp.dma_start(adj_i[:, :, :], pick(adj_u, st, v0)).then_inc(adj_in, 16)
                if v3 is not None:
                    sp.wait_ge(r_out, 16 * st.nth0(v3))
                    sp.wait_ge(m_out, 16 * st.nth0(v3))
                    sp.wait_ge(x_made, st.nth0(v3))
                    sp.dma_start(pick(xs_u, st, v3), made(v3)[:, :, :]).then_inc(h_out, 16)
                if v2 is not None and v2 < CH:
                    if v2:
                        sp.wait_ge(h_out, 16 * st.nth0(v2 - 1))
                    sp.dma_start(xin[1][:, :, :], pick(x_u, st, v2)).then_inc(xr_in, 16)
                if v0 is not None:
                    sp.wait_ge(masks_ready, st.nth0(v0))
                    sp.dma_start(pick(m_u, st, v0), m_new[:, :, :].bitcast(I32)).then_inc(m_out, 16)
                if v2 is not None:
                    sp.wait_ge(x1_ready, st.nth0(v2))
                    sp.dma_start(pick(r_u, st, v2), elu_r[:, :, :]).then_inc(r_out, 16)

            steps(sp, body)
            sp.wait_ge(y_out, 16 * U)
            sp.wait_ge(r_out, 16 * G)
            sp.wait_ge(h_out, 16 * G)
            sp.wait_ge(m_out, 16 * G)

        @block.tensor
        def _(pe):
            pe.wait_ge(const_in, 16 * 12)
            for j in range(2):
                mm = pe.matmul(ps_s[:, j * D:(j + 1) * D], a_col[:, j:j + 1].to_broadcast((O, P)), wfc,
                               start=True, stop=True)
            mm.then_inc(v_ps, 1)
            for l in range(L):
                pe.wait_ge(w_in[l], 16 * 2 * K1)
                for c in range(C):
                    for k in range(K1):
                        mm = pe.matmul(ps_u[0][:, l * C + c:l * C + c + 1],
                                       raw1[l % 2][k].rearrange("p t d -> p (t d)")[:, c * P:(c + 1) * P],
                                       beta1_col[:, l, k:k + 1], start=(k == 0), stop=(k == K1 - 1))
                mm.then_inc(b1_ps, 1)
            pe.wait_ge(b1_ready, 1)
            pe.wait_ge(w_ready, 2 * K1 * L)
            pe.wait_ge(w_hi_ready, 2 * K1 * L)
            pe.wait_ge(ident_ready, 2)

            def score_rows(scores, mask, dot, done):
                for t in range(T):
                    pe.matmul(scores[:, t * P:(t + 1) * P], dot[:, 1, t:t + 1].to_broadcast((P, P)), ident[:, :],
                              is_transpose=True, start=(t == 0), stop=True, skip_group_check=True)
                pe.matmul(scores[:, :], ident_b[:, :], mask.rearrange("p t m -> p (t m)"),
                          start=False, stop=True, skip_group_check=True).then_inc(done, 1)

            def bank_read(st, s, c):
                if c in POOL_LOW:
                    pe.wait_ge(gelu_done, st.nth(s, C, c + 1))
                else:
                    pe.wait_ge(g_lo_ready, st.nth(s, C - 2, c + 1 - sum(b < c for b in POOL_LOW)))

            def turn_weights(dst, done):
                for t in range(T):
                    mm = pe.transpose(dst[:, t * P:(t + 1) * P], e1[:, t, :], ident[:, :])
                mm.then_inc(done, 1)

            def aggregate(weights, rows, done):
                for t in range(T):
                    pe.matmul(ps_u[t // 2][:, t % 2 * D:(t % 2 + 1) * D], weights[:, t, :], rows[:, t, :],
                              start=True, stop=True).then_inc(done, 1)

            def body(st):
                s = st.s
                v1, v2 = middle(s), late(s)
                l = layer(s)

                def hidden(c):
                    if not live(s):
                        return
                    if c == 0:
                        pe.wait_ge(zt_hi_ready, st.nth(s))
                        pe.wait_ge(zt_lo_ready, st.nth(s))
                    if bank[turn[c]] in ps_y and c < 4 and live(s - 1):
                        pe.wait_ge(v_done, st.nth(s - 1, 2, turn[c] - 1))
                    if c >= 4:
                        bank_read(st, s, turn[:4].index(turn[c]))
                    n = 0
                    for k in range(K1):
                        for w, z in ((w1_hi, zt_hi), (w1_hi, zt_lo), (w1_lo, zt_hi)):
                            mm = pe.matmul(bank[turn[c]][:, :], w[:, l, k, c * P:(c + 1) * P], z[:, k, :],
                                           start=(n == 0), stop=(n == 3 * K1 - 1))
                            n += 1
                    mm.then_inc(ff1_done, 1)

                def second(r):
                    if not live(s):
                        return
                    if r in (0, 2):
                        bank_read(st, s, 5 if r == 0 else 7)
                    for c in range(C):
                        if r == 0:
                            low_done(pe, st, s, c)
                        y = ps_y[r // 2][:, r % 2 * D:(r % 2 + 1) * D]
                        for n, (g, w) in enumerate(((g_hi, w2_hi), (g_hi, w2_lo), (g_lo, w2_hi))):
                            mm = pe.matmul(y, g[:, c, r * P:(r + 1) * P], w[:, l, c, :],
                                           start=(c == 0 and n == 0), stop=(c == C - 1 and n == 2))
                    mm.then_inc(ff2_done, 1)

                if v2 is not None:
                    pe.wait_ge(e0_ready, st.nth0(v2))
                    turn_weights(ps_s0, et0_ps)
                hidden(0)
                if live(s + 1):
                    pe.wait_ge(et_ready, st.nth(s + 1))
                    if late(s - 1) is not None:
                        pe.wait_ge(elu_parts, st.nth0(late(s - 1)))
                    if live(s):
                        pe.wait_ge(zt_lo_ready, st.nth(s))
                    aggregate(et, xb[(s + 1) % 2], agg_done)
                hidden(1)
                if live(s + 2):
                    pe.wait_ge(dots_ready, st.nth(s + 2, 2 * T))
                    pe.wait_ge(m_in, 16 * st.nth(s + 2))
                    if live(s + 1):
                        pe.wait_ge(et_ready, st.nth(s + 1))
                    score_rows(ps_s, m1[s % 2][:, :, :], dots[s % 2], scores_ready)
                if v1 is not None:
                    pe.wait_ge(dots0_ready, st.nth0(v1, 2 * T))
                    pe.wait_ge(masks0_ready, st.nth0(v1))
                    if v1:
                        pe.wait_ge(et0_ready, st.nth0(v1 - 1))
                    score_rows(ps_s0, m0[:, :, :], dots0, scores0_ready)
                for c in range(2, C):
                    hidden(c)
                if live(s + 1):
                    pe.wait_ge(z_ready, st.nth(s + 1))
                    for k in range(K1):
                        for t in range(T):
                            mm = pe.transpose(ps_u[k][:, t * P:(t + 1) * P], ub[:, t, k * P:(k + 1) * P], ident[:, :])
                    mm.then_inc(zt_ps, 1)
                second(0)
                if v2 is not None:
                    pe.wait_ge(et0_ready, st.nth0(v2))
                    if live(s + 1):
                        pe.wait_ge(zt_lo_ready, st.nth(s + 1))
                    elif late(s - 1) is not None:
                        pe.wait_ge(elu_parts, st.nth0(late(s - 1)))
                    aggregate(et0, h0[v2 % 2], agg0_done)
                second(1)
                second(2)
                if live(s + 2):
                    pe.wait_ge(e_ready, st.nth(s + 2))
                    turn_weights(ps_s, et_ps)
                second(3)

            steps(pe, body)

        @block.scalar
        def _(act):
            for l in range(L):
                act.wait_ge(const_in, 16 * 12)
                act.wait_ge(w_in[l], 16 * 2 * K1)
                for k in range(K1):
                    act.activation(w1_hi[:, l, k, :], raw1[l % 2][k].rearrange("p t d -> p (t d)"), ACT.Copy,
                                   scale=g1_col[:, l, k:k + 1]).then_inc(w_hi_ready, 1)
                    act.activation(w2_hi[:, l, k * HC:(k + 1) * HC, :], raw2[l % 2][k][:, :, :],
                                   ACT.Copy).then_inc(w_hi_ready, 1)
            act.wait_ge(w_ready, 2 * K1 * L)
            act.wait_ge(b1_ready, 1)

            def exps(scores, cols):
                for t in range(T):
                    src = scores[:, t * P:(t + 1) * P]
                    act.activation(e1[:, t, :], src, ACT.Exp, bias=cols[:, 0, t:t + 1])
                    a = act.activation(e2[:, t, :], src, ACT.Exp, bias=cols[:, 1, t:t + 1], scale=SLOPE)
                return a

            def norm_relu(dst, src, rs, nm):
                for t in range(T):
                    a = act.activation(dst[:, t, :], src[:, t, :], ACT.Relu, bias=nm[:, t:t + 1], scale=rs[:, t:t + 1])
                return a

            def body(st):
                s = st.s
                v0, v1, v2, v3 = early(s), middle(s), late(s), end(s)
                if v2 is not None:
                    act.wait_ge(et0_ps, st.nth0(v2))
                    if v2:
                        act.wait_ge(agg0_done, st.nth0(v2 - 1, T))
                    act.activation(et0.rearrange("p t m -> p (t m)"), ps_s0[:, :], ACT.Copy).then_inc(et0_ready, 1)
                if live(s):
                    for c in range(C):
                        act.wait_ge(ff1_done, st.nth(s, C, c + 1))
                        block_in = bank[turn[c]][:, :]
                        bias = b1_eff[:, layer(s), c:c + 1]
                        act.activation(g_hi[:, c, :], block_in, ACT.Gelu, bias=bias).then_inc(g_hi_ready, 1)
                        if c not in POOL_LOW:
                            act.wait_ge(g_hi_ready, st.nth(s, C, c + 1))
                            full = block_in
                        else:
                            full = g_full
                            if c == POOL_LOW[0] and early(s - 1) is not None:
                                act.wait_ge(masks_ready, st.nth0(early(s - 1)))
                            elif c == POOL_LOW[1]:
                                act.wait_ge(g_lo_pool, st.nth(s, 2, 1))
                        act.activation(full, block_in, ACT.Gelu, bias=bias).then_inc(gelu_done, 1)
                if live(s + 1):
                    act.wait_ge(zt_ps, st.nth(s + 1))
                    for k in range(K1):
                        a = act.activation(zt_hi[:, k, :], ps_u[k][:, :], ACT.Copy)
                    a.then_inc(zt_hi_ready, 1)
                if live(s + 2):
                    act.wait_ge(cc_ready, st.nth(s + 2))
                    exps(ps_s, cc).then_inc(e12_ready, 1)
                if v3 is not None:
                    act.wait_ge(nm3_ready, st.nth0(v3))
                    norm_relu(made(v3), elu_r, rs3, nm3).then_inc(x_made, 1)
                if v0 is not None:
                    act.wait_ge(nm4_ready, st.nth0(v0))
                    if v0 >= 2:
                        act.wait_ge(agg0_done, st.nth0(v0 - 2, T))
                    if v0 >= CH + 2:
                        act.wait_ge(h_out, 16 * st.nth0(v0 - 2))
                    norm_relu(h0[v0 % 2], xin[0], rs4, nm4).then_inc(h0_ready, 1)
                if v2 is not None:
                    act.wait_ge(rinv0_ready, st.nth0(v2))
                    if v2:
                        act.wait_ge(r_out, 16 * st.nth0(v2 - 1))
                        act.wait_ge(x_made, st.nth0(v2 - 1))
                    if live(s - 1):
                        act.wait_ge(z2_ready, st.nth(s - 1))
                    for t in range(T):
                        if t % 2 == 0:
                            act.wait_ge(agg0_done, st.nth0(v2, T, t + 2))
                        src = ps_u[t // 2][:, t % 2 * D:(t % 2 + 1) * D]
                        act.activation(elu_e[:, t, :], src, ACT.Exp, scale=rinv0[:, t:t + 1])
                        a = act.activation(elu_r[:, t, :], src, ACT.Relu, scale=rinv0[:, t:t + 1])
                    a.then_inc(elu_parts, 1)
                if live(s + 2):
                    act.wait_ge(et_ps, st.nth(s + 2))
                    if live(s + 1):
                        act.wait_ge(agg_done, st.nth(s + 1, T))
                    act.activation(et.rearrange("p t m -> p (t m)"), ps_s[:, :], ACT.Copy).then_inc(et_ready, 1)
                if v1 is not None:
                    act.wait_ge(cc0_ready, st.nth0(v1))
                    if live(s + 2):
                        act.wait_ge(et_ps, st.nth(s + 2))
                    exps(ps_s0, cc0).then_inc(e12_0_ready, 1)

            steps(act, body)

        @block.vector
        def _(dve):
            done = [0]

            def link(ins):
                done[0] += 1
                ins.then_inc(pro, 1)
                dve.wait_ge(pro, done[0])

            link(dve.memset(neg_half[:, :], -0.5))
            dve.wait_ge(const_in, 16 * 12)
            link(dve.tensor_tensor(bb_row[:, :, :], bb_row[:, :, :], h0[0][:, 0:L, :], ALU.add))
            dve.wait_ge(v_ps, 1)
            link(dve.tensor_copy(v_row.rearrange("p a d -> p (a d)"), ps_s[:, :]))
            for l in range(L):
                dve.wait_ge(w_in[l], 16 * 2 * K1)
                for k in range(K1):
                    dve.wait_ge(w_hi_ready, 2 * (K1 * l + k) + 1)
                    dve.scalar_tensor_tensor(out=w1_lo[:, l, k, :], in0=raw1[l % 2][k].rearrange("p t d -> p (t d)"),
                                             scalar=g1_col[:, l, k:k + 1], in1=w1_hi[:, l, k, :].bitcast(F32),
                                             op0=ALU.mult, op1=ALU.subtract).then_inc(w_ready, 1)
                    dve.wait_ge(w_hi_ready, 2 * (K1 * l + k) + 2)
                    dve.tensor_tensor(w2_lo[:, l, k * HC:(k + 1) * HC, :], raw2[l % 2][k][:, :, :],
                                      w2_hi[:, l, k * HC:(k + 1) * HC, :].bitcast(F32),
                                      ALU.subtract).then_inc(w_ready, 1)
            dve.wait_ge(b1_ps, L)
            dve.tensor_tensor(b1_eff.rearrange("p l c -> p (l c)"), ps_u[0][:, 0:L * C],
                              b1_col.rearrange("p l c -> p (l c)"), ALU.add).then_inc(b1_ready, 1)

            def branch_biases(nth, u, scores, sm, dot, cols, per_head, steps_sem, ready):
                dve.tensor_reduce(sm[:, 0, :], scores.rearrange("p (t m) -> p t m", t=T), AX, ALU.max)
                if per_head is None:
                    dve.tensor_copy(sm[:, 1, :], dot[:, 0, :]).then_inc(steps_sem, 1)
                else:
                    dve.tensor_scalar(sm[:, 1, :], dot[:, 0, :], per_head, None, ALU.add).then_inc(steps_sem, 1)
                dve.wait_ge(steps_sem, nth(u, 3, 1))
                dve.tensor_tensor(sm[:, 2, :], sm[:, 0, :], sm[:, 1, :], ALU.add).then_inc(steps_sem, 1)
                dve.wait_ge(steps_sem, nth(u, 3, 2))
                dve.scalar_tensor_tensor(out=sm[:, 3, :], in0=sm[:, 2, :], scalar=SLOPE, in1=sm[:, 2, :],
                                         op0=ALU.mult, op1=ALU.max).then_inc(steps_sem, 1)
                dve.wait_ge(steps_sem, nth(u, 3, 3))
                dve.tensor_tensor(cols[:, 0, :], sm[:, 1, :], sm[:, 3, :], ALU.subtract)
                dve.scalar_tensor_tensor(out=cols[:, 1, :], in0=sm[:, 1, :], scalar=SLOPE, in1=sm[:, 3, :],
                                         op0=ALU.mult, op1=ALU.subtract).then_inc(ready, 1)

            def weights(nth, u, rs, ri, e12, e_done, r_done):
                dve.wait_ge(e12, nth(u))
                for t in range(T):
                    ins = dve.scalar_tensor_tensor(out=e1[:, t, :], in0=e1[:, t, :], scalar=1.0, in1=e2[:, t, :],
                                                   op0=ALU.mult, op1=ALU.max, accum_out=rs[:, t:t + 1])
                ins.then_inc(e_done, 1)
                dve.wait_ge(e_done, nth(u))
                dve.reciprocal(ri[:, :], rs[:, :]).then_inc(r_done, 1)

            def row_dots(nth, u, dot, rows, vec, ready):
                for t in range(T):
                    for j in range(2):
                        if t:
                            dve.wait_ge(ready, nth(u, 2 * T, 2 * t + j - 1))
                        dve.tensor_tensor_reduce(junk[:, j, :], rows[:, t, :], vec(j), 1.0, 0.0,
                                                 ALU.mult, ALU.add, dot[:, j, t:t + 1]).then_inc(ready, 1)

            def statistics(rows, st_t, ready):
                for t in range(T):
                    ins = dve.bn_stats(st_t[:, t, :], rows[:, t, :])
                ins.then_inc(ready, 1)

            def variance(nth, u, st_t, mv, ve, mv_ready, ve_ready):
                for t in range(T):
                    ins = dve.bn_aggr(mv[:, t, :], st_t[:, t, :])
                ins.then_inc(mv_ready, 1)
                dve.wait_ge(mv_ready, nth(u))
                dve.tensor_scalar(ve[:, :], mv[:, :, 1], EPS, None, ALU.add).then_inc(ve_ready, 1)

            def normalise(dst, rows, mv, rs, ready):
                for t in range(T):
                    ins = dve.tensor_scalar(dst[:, t, :], rows[:, t, :], mv[:, t, 0:1], rs[:, t:t + 1],
                                            ALU.subtract, ALU.mult)
                ins.then_inc(ready, 1)

            def body(st):
                s = st.s
                v0, v1, v2, v3 = early(s), middle(s), late(s), end(s)

                def g_low(c):
                    if live(s) and c not in POOL_LOW:
                        dve.wait_ge(gelu_done, st.nth(s, C, c + 1))
                        dve.tensor_tensor(g_lo[:, c, :], bank[turn[c]][:, :], g_hi[:, c, :].bitcast(F32),
                                          ALU.subtract).then_inc(g_lo_ready, 1)

                if live(s - 1):
                    dve.wait_ge(h_ready, st.nth(s - 1))
                    if live(s - 2):
                        dve.wait_ge(z2_ready, st.nth(s - 2))
                    if late(s - 1) is not None:
                        dve.wait_ge(x1_ready, st.nth0(late(s - 1)))
                    for r in range(2):
                        dve.wait_ge(ff2_done, st.nth(s - 1, T, 2 * r + 2))
                        dve.tensor_tensor(vb[:, 2 * r:2 * r + 2, :], ps_y[r].rearrange("p (t d) -> p t d", d=D),
                                          hb[(s - 1) % 2][:, 2 * r:2 * r + 2, :], ALU.add).then_inc(v_done, 1)
                g_low(0)
                if live(s + 1):
                    dve.wait_ge(rinv_ready, st.nth(s + 1))
                    if live(s):
                        dve.wait_ge(h_ready, st.nth(s))
                        dve.wait_ge(zt_ps, st.nth(s))
                    if live(s + 2):
                        dve.wait_ge(dots_ready, st.nth(s + 2, 2 * T))
                    if early(s - 1) is not None:
                        dve.wait_ge(dots0_ready, st.nth0(early(s - 1), 2 * T))
                    for t in range(T):
                        if t % 2 == 0:
                            dve.wait_ge(agg_done, st.nth(s + 1, T, t + 2))
                        ins = dve.scalar_tensor_tensor(
                            out=ub[:, t, :], in0=ps_u[t // 2][:, t % 2 * D:(t % 2 + 1) * D],
                            scalar=rinv[:, t:t + 1], in1=xb[(s + 1) % 2][:, t, :], op0=ALU.mult, op1=ALU.add)
                    ins.then_inc(u_done, 1)
                    dve.wait_ge(u_done, st.nth(s + 1))
                    statistics(ub, st1, st1_ready)
                    dve.wait_ge(st1_ready, st.nth(s + 1))
                g_low(1)
                if live(s + 1):
                    variance(st.nth, s + 1, st1, mv1, ve1, mv1_ready, ve1_ready)
                if live(s + 2):
                    dve.wait_ge(scores_ready, st.nth(s + 2))
                    if live(s + 1):
                        dve.wait_ge(e12_ready, st.nth(s + 1))
                    l2 = layer(s + 2)
                    branch_biases(st.nth, s + 2, ps_s, small, dots[s % 2], cc, ab_col[:, l2:l2 + 1], max_steps, cc_ready)
                g_low(3)
                if live(s + 1):
                    dve.wait_ge(rs1_ready, st.nth(s + 1))
                    normalise(ub, ub, mv1, rs1, z_ready)
                g_low(4)
                if live(s - 1):
                    dve.wait_ge(v_done, st.nth(s - 1, 2))
                    statistics(vb, st2, st2_ready)
                    dve.wait_ge(st2_ready, st.nth(s - 1))
                g_low(6)
                if live(s - 1):
                    variance(st.nth, s - 1, st2, mv2, ve2, mv2_ready, ve2_ready)
                g_low(7)
                if v3 is not None:
                    dve.wait_ge(rs3_ready, st.nth0(v3))
                    dve.scalar_tensor_tensor(out=nm3[:, :], in0=mv3[:, :, 0], scalar=-1.0, in1=rs3[:, :],
                                             op0=ALU.mult, op1=ALU.mult).then_inc(nm3_ready, 1)
                if live(s + 1):
                    dve.wait_ge(zt_hi_ready, st.nth(s + 1))
                    for k in range(K1):
                        ins = dve.tensor_tensor(zt_lo[:, k, :], ps_u[k][:, :], zt_hi[:, k, :].bitcast(F32),
                                                ALU.subtract)
                    ins.then_inc(zt_lo_ready, 1)
                if live(s - 1):
                    dve.wait_ge(rs2_ready, st.nth(s - 1))
                    if live(s - 2):
                        dve.wait_ge(y_out, 16 * st.nth(s - 2))
                    normalise(xo, vb, mv2, rs2, z2_ready)
                if v0 is not None:
                    dve.wait_ge(xin_in, 16 * st.nth0(v0))
                    statistics(xin[0], st4, st4_ready)
                    dve.wait_ge(st4_ready, st.nth0(v0))
                if live(s + 2):
                    weights(st.nth, s + 2, rsum, rinv, e12_ready, e_ready, rinv_ready)
                if v0 is not None:
                    variance(st.nth0, v0, st4, mv4, ve4, mv4_ready, ve4_ready)
                if v1 is not None:
                    dve.wait_ge(scores0_ready, st.nth0(v1))
                    branch_biases(st.nth0, v1, ps_s0, small0, dots0, cc0, None, max0_steps, cc0_ready)
                if live(s + 3):
                    dve.wait_ge(x_in, 16 * st.nth(s + 3))
                    if live(s + 1):
                        dve.wait_ge(h_scaled, st.nth(s + 1))
                        dve.wait_ge(zt_ps, st.nth(s + 1))
                    l3 = layer(s + 3)
                    row_dots(st.nth, s + 3, dots[(s + 3) % 2], xb[(s + 3) % 2],
                             lambda j: aw_row[:, l3, j * D:(j + 1) * D], dots_ready)
                if v0 is not None:
                    dve.wait_ge(rs4_ready, st.nth0(v0))
                    dve.scalar_tensor_tensor(out=nm4[:, :], in0=mv4[:, :, 0], scalar=-1.0, in1=rs4[:, :],
                                             op0=ALU.mult, op1=ALU.mult).then_inc(nm4_ready, 1)
                if v2 is not None:
                    dve.wait_ge(elu_parts, st.nth0(v2))
                    dve.scalar_tensor_tensor(out=elu_e.rearrange("p t d -> p (t d)"),
                                             in0=elu_e.rearrange("p t d -> p (t d)"), scalar=1.0,
                                             in1=elu_r.rearrange("p t d -> p (t d)"),
                                             op0=ALU.min, op1=ALU.add).then_inc(elu_sum, 1)
                    dve.wait_ge(elu_sum, st.nth0(v2))
                    if v2 < CH:
                        dve.wait_ge(xr_in, 16 * st.nth0(v2))
                    dve.scalar_tensor_tensor(out=elu_r.rearrange("p t d -> p (t d)"),
                                             in0=elu_e.rearrange("p t d -> p (t d)"), scalar=-1.0,
                                             in1=residual_x(v2).rearrange("p t d -> p (t d)"),
                                             op0=ALU.add, op1=ALU.add).then_inc(x1_ready, 1)
                    dve.wait_ge(x1_ready, st.nth0(v2))
                    statistics(elu_r, st3, st3_ready)
                    dve.wait_ge(st3_ready, st.nth0(v2))
                    dve.tensor_copy(small0[:, 4, :], neg_half[:, :])
                    variance(st.nth0, v2, st3, mv3, ve3, mv3_ready, ve3_ready)
                if v1 is not None:
                    weights(st.nth0, v1, rsum0, rinv0, e12_0_ready, e0_ready, rinv0_ready)
                if v0 is not None:
                    dve.wait_ge(h0_ready, st.nth0(v0))
                    if live(s + 3):
                        dve.wait_ge(dots_ready, st.nth(s + 3, 2 * T))
                    row_dots(st.nth0, v0, dots0, h0[v0 % 2], lambda j: v_row[:, j, :], dots0_ready)

            steps(dve, body)

        @block.gpsimd
        def _(pool):
            pool.memset(ident[:, :], 0.0).then_inc(zeroed, 1)
            pool.memset(ident_b[:, :], 0.0).then_inc(zeroed, 1)
            pool.wait_ge(zeroed, 2)
            for m in (ident, ident_b):
                pool.affine_select(out=m[:, :], in_=m[:, :], compare_op=ALU.not_equal, fill=1.0, base=0,
                                   pattern=[[-1, P]], channel_multiplier=1).then_inc(ident_ready, 1)
            pool.wait_ge(ident_ready, 2)
            pool.tensor_copy(eye_i[:, :], ident[:, :]).then_inc(ident_ready, 1)
            pool.wait_ge(ident_ready, 3)
            pool.wait_ge(b1_ready, 1)

            def all_graphs(row):
                return row.unsqueeze(1).to_broadcast((P, T, D))

            def take_waits():
                pool.tensor_tensor(spare[:, :], neg_half[:, 0:1], neg_half[:, 0:1], ALU.mult)

            def inverse_root(value, ve, rs, ve_ready, rs_ready):
                pool.wait_ge(ve_ready, value)
                pool.tensor_tensor(rs[:, :], ve[:, :], neg_half[:, :], ALU.pow).then_inc(rs_ready, 1)

            def body(st):
                s = st.s
                v0, v2 = early(s), late(s)
                if live(s - 2):
                    l = layer(s - 2)
                    last = l == L - 1
                    pool.wait_ge(z2_ready, st.nth(s - 2))
                    pool.tensor_tensor(xo[:, :, :], xo[:, :, :], all_graphs(g2_row[:, l, :]),
                                       ALU.mult).then_inc(xo_scaled, 1)
                    pool.wait_ge(xo_scaled, st.nth(s - 2))
                    pool.tensor_tensor(xo[:, :, :], xo[:, :, :], all_graphs(beta2_row[:, l, :]),
                                       ALU.add).then_inc(xo_shifted if last else xo_ready, 1)
                    if last:
                        pool.wait_ge(xo_shifted, st.nth0(group(s - 2)))
                        pool.wait_ge(r_in, 16 * st.nth0(group(s - 2)))
                        pool.tensor_tensor(xo[:, :, :], xo[:, :, :], xin[1][:, :, :], ALU.add).then_inc(xo_ready, 1)
                if live(s + 1):
                    inverse_root(st.nth(s + 1), ve1, rs1, ve1_ready, rs1_ready)
                if live(s):
                    for c in POOL_LOW:
                        pool.wait_ge(gelu_done, st.nth(s, C, c + 1))
                        pool.tensor_tensor(g_lo[:, c, :], g_full, g_hi[:, c, :].bitcast(F32),
                                           ALU.subtract).then_inc(g_lo_pool, 1)
                if live(s - 1):
                    inverse_root(st.nth(s - 1), ve2, rs2, ve2_ready, rs2_ready)
                if live(s + 1):
                    l = layer(s + 1)
                    pool.wait_ge(z_ready, st.nth(s + 1))
                    if live(s - 1):
                        pool.wait_ge(v_done, st.nth(s - 1, 2))
                    h = hb[(s + 1) % 2]
                    pool.tensor_tensor(h[:, :, :], ub[:, :, :], all_graphs(g1_row[:, l, :]), ALU.mult).then_inc(h_scaled, 1)
                    pool.wait_ge(h_scaled, st.nth(s + 1))
                    pool.tensor_tensor(h[:, :, :], h[:, :, :], all_graphs(bb_row[:, l, :]), ALU.add).then_inc(h_ready, 1)
                if v0 is not None:
                    inverse_root(st.nth0(v0), ve4, rs4, ve4_ready, rs4_ready)
                    pool.wait_ge(adj_in, 16 * st.nth0(v0))
                    if v0:
                        pool.wait_ge(scores0_ready, st.nth0(v0 - 1))
                    take_waits()
                    pool.tensor_scalar(m0[:, :, :], adj_i[:, :, :], 0.0, -BIG,
                                       ALU.is_equal, ALU.mult).then_inc(masks0_ready, 1)
                    pool.wait_ge(masks0_ready, st.nth0(v0))
                    pool.tensor_tensor(adj_i[:, :, :], adj_i[:, :, :], eye_i[:, :].unsqueeze(1).to_broadcast((P, T, P)),
                                       ALU.add).then_inc(masks_sum, 1)
                    pool.wait_ge(masks_sum, st.nth0(v0))
                    if v0:
                        pool.wait_ge(m_out, 16 * st.nth0(v0 - 1))
                    take_waits()
                    pool.tensor_scalar(m_new[:, :, :], adj_i[:, :, :], 0.0, -BIG,
                                       ALU.is_le, ALU.mult).then_inc(masks_ready, 1)
                if v2 is not None:
                    inverse_root(st.nth0(v2), ve3, rs3, ve3_ready, rs3_ready)

            steps(pool, body)


_INS = ["x", "adj", "L0_gnn_W_fc", "L0_gnn_W_attn", "L1_gnn_attn_w", "L1_gnn_attn_b", "L1_gnn_W1", "L1_gnn_b1",
        "L1_gnn_W2", "L1_gnn_b2", "L1_gnn_g1", "L1_gnn_beta1", "L1_gnn_g2", "L1_gnn_beta2"]


def kernel(**inputs):
    import numpy as np
    import concourse.bacc as bacc
    from concourse import mybir as mb
    from concourse.bass_utils import run_bass_kernel_spmd

    nc = bacc.Bacc("TRN2", target_bir_lowering=False, num_devices=1, dynamic_dma_scratch_size=1024)
    arrays, args = {}, []
    for name in _INS:
        a = np.ascontiguousarray(inputs[name])
        arrays[f"in_{name}"] = a
        args.append(nc.dram_tensor(f"in_{name}", a.shape, mb.dt.from_np(a.dtype), kind="ExternalInput").ap())
    out = nc.dram_tensor("out", inputs["x"].shape, mb.dt.float32, kind="ExternalOutput").ap()
    build(nc, *args, out)
    r = run_bass_kernel_spmd(nc, [arrays], core_ids=[0])
    return r.results[0]["out"]
```

```python
from contextlib import ExitStack

import concourse.bass as bass
from concourse import mybir

ALU = mybir.AluOpType
ACT = mybir.ActivationFunctionType
AX = mybir.AxisListType.X
F32 = mybir.dt.float32
F32R = mybir.dt.float32r
BF16 = mybir.dt.bfloat16
I32 = mybir.dt.int32

P = 128
T = 4
EPS = 1e-5
SLOPE = 0.2
BIG = 2.0 ** 100


class Step:

    def __init__(self, s, off=0, off0=0):
        self.s, self.off, self.off0 = s, off, off0

    def nth(self, unit, per=1, j=None):
        return unit * per + (per if j is None else j) + self.off * per

    def nth0(self, group, per=1, j=None):
        return group * per + (per if j is None else j) + self.off0 * per


def build(nc, x, adj, w_fc, w_attn0, attn_w, attn_b, w1, b1, w2, b2, g1, beta1, g2, beta2, out):
    B, N, D = x.shape
    L = w1.shape[0]
    F = w1.shape[2]
    O = w_fc.shape[0]
    K1 = D // P
    C = F // P
    G = B // T
    CH = 8
    PER = L * CH
    FILL = 7
    U = L * G
    assert N == P and K1 == 2 and C == 8 and L == 3 and G % CH == 0

    def layer(n):
        return n % PER // CH

    def group(n):
        return n // PER * CH + n % CH

    x_u = x.rearrange("(g t) n d -> g n t d", t=T)
    adj_u = adj.rearrange("(g t) n m -> g n t m", t=T)
    out_u = out.rearrange("(g t) n d -> g n t d", t=T)
    xs_u = nc.dram_tensor("x_scratch", (L * G, P, T, D), F32, kind="Internal").ap()
    r_u = nc.dram_tensor("r_scratch", (G, P, T, D), F32, kind="Internal").ap()
    m_u = nc.dram_tensor("m_scratch", (G, P, T, P // 2), I32, kind="Internal").ap()

    ctx = ExitStack()
    with ctx:
        def sb(name, shape, dt=F32):
            return ctx.enter_context(nc.sbuf_tensor(name, shape, dt))

        def sem(name):
            return ctx.enter_context(nc.semaphore(name))

        w1_hi = sb("w1_hi", [P, L, K1, F], F32R)
        w1_lo = sb("w1_lo", [P, L, K1, F], F32R)
        w2_hi = sb("w2_hi", [P, L, C, D], F32R)
        w2_lo = sb("w2_lo", [P, L, C, D], F32R)
        b1_eff = sb("b1_eff", [P, L, C])
        g1_row = sb("g1_row", [P, L, D])
        bb_row = sb("bb_row", [P, L, D])
        g2_row = sb("g2_row", [P, L, D])
        beta2_row = sb("beta2_row", [P, L, D])
        aw_row = sb("aw_row", [P, L, 2 * D])
        ab_col = sb("ab_col", [P, L])
        g1_col = sb("g1_col", [P, L, K1])
        beta1_col = sb("beta1_col", [P, L, K1])
        b1_col = sb("b1_col", [P, L, C])
        a_col = sb("a_col", [O, 2])
        v_row = sb("v_row", [P, 2, D])
        ident = sb("ident", [P, P])
        ident_b = sb("ident_b", [P, P], BF16)
        eye_i = sb("eye_i", [P, P], I32)
        neg_half = sb("neg_half", [P, T])
        spare = sb("spare", [P, 2])

        xb = [sb(f"xb{i}", [P, T, D]) for i in range(2)]
        hb = [sb(f"hb{i}", [P, T, D]) for i in range(2)]
        zt_hi = sb("zt_hi", [P, K1, T * P], F32R)
        zt_lo = sb("zt_lo", [P, K1, T * P], F32R)
        g_hi = sb("g_hi", [P, C, T * P], F32R)
        g_lo = sb("g_lo", [P, C, T * P], F32R)
        e1 = sb("e1", [P, T, P])
        e2 = sb("e2", [P, T, P])
        et = sb("et", [P, T, P])
        wfc = et[0:O, :, :].rearrange("p t m -> p (t m)")[:, 0:D]
        ub = sb("ub", [P, T, D])
        vb = sb("vb", [P, T, D])
        xo = sb("xo", [P, T, D])
        adj_i = sb("adj_i", [P, T, P], I32)
        g_full = adj_i.rearrange("p t m -> p (t m)").bitcast(F32)
        m1 = [sb(f"m1_{i}", [P, T, P], BF16) for i in range(2)]
        m_new = sb("m_new", [P, T, P], BF16)
        dots = [sb(f"dots_{i}", [P, 2, T]) for i in range(2)]
        junk = ub
        small = sb("small", [P, 5, T])
        cc = sb("cc", [P, 2, T])
        rsum = sb("rsum", [P, T])
        rinv = sb("rinv", [P, T])
        st1 = sb("st1", [P, T, 6])
        mv1 = sb("mv1", [P, T, 2])
        ve1 = sb("ve1", [P, T])
        rs1 = sb("rs1", [P, T])
        st2 = sb("st2", [P, T, 6])
        mv2 = sb("mv2", [P, T, 2])
        ve2 = sb("ve2", [P, T])
        rs2 = sb("rs2", [P, T])

        xin = [sb(f"xin{i}", [P, T, D]) for i in range(2)]
        h0 = [sb(f"h0_{i}", [P, T, D]) for i in range(2)]
        elu_e = vb
        elu_r = sb("elu_r", [P, T, D])
        et0 = sb("et0", [P, T, P])
        m0 = sb("m0", [P, T, P], BF16)
        dots0 = sb("dots0", [P, 2, T])
        small0 = sb("small0", [P, 5, T])
        cc0 = sb("cc0", [P, 2, T])
        rsum0 = sb("rsum0", [P, T])
        rinv0 = sb("rinv0", [P, T])
        st3 = sb("st3", [P, T, 6])
        mv3 = sb("mv3", [P, T, 2])
        ve3 = sb("ve3", [P, T])
        rs3 = sb("rs3", [P, T])
        nm3 = sb("nm3", [P, T])
        st4 = sb("st4", [P, T, 6])
        mv4 = sb("mv4", [P, T, 2])
        ve4 = sb("ve4", [P, T])
        rs4 = sb("rs4", [P, T])
        nm4 = sb("nm4", [P, T])

        HC = C // 2
        raw1 = [xb, [ub, vb]]
        raw2 = [hb, [xo, elu_r]]

        bank = [ctx.enter_context(nc.psum_tensor(f"bank{i}", [P, 512], F32)) for i in range(4)]
        ps_y = bank[2:4]
        turn = [0, 1, 2, 3, 0, 2, 1, 3]
        ps_s = ctx.enter_context(nc.psum_tensor("ps_s", [P, T * P], F32))
        ps_s0 = ctx.enter_context(nc.psum_tensor("ps_s0", [P, T * P], F32))
        ps_u = [ctx.enter_context(nc.psum_tensor(f"ps_u{i}", [P, 512], F32)) for i in range(2)]

        const_in = sem("const_in")
        rows_in = sem("rows_in")
        w_in = [sem(f"w_in{l}") for l in range(L)]
        zeroed = sem("zeroed")
        ident_ready = sem("ident_ready")
        b1_ps = sem("b1_ps")
        v_ps = sem("v_ps")
        pro = sem("pro")
        w_hi_ready = sem("w_hi_ready")
        w_ready = sem("w_ready")
        b1_ready = sem("b1_ready")

        adj_in = sem("adj_in")
        x_in = sem("x_in")
        y_out = sem("y_out")
        r_in = sem("r_in")
        m_in = sem("m_in")
        m_out = sem("m_out")
        h_out = sem("h_out")
        xin_in = sem("xin_in")
        xr_in = sem("xr_in")
        r_out = sem("r_out")

        masks_sum = sem("masks_sum")
        masks_ready = sem("masks_ready")
        dots_ready = sem("dots_ready")
        scores_ready = sem("scores_ready")
        max_steps = sem("max_steps")
        cc_ready = sem("cc_ready")
        e12_ready = sem("e12_ready")
        e_ready = sem("e_ready")
        rinv_ready = sem("rinv_ready")
        et_ps = sem("et_ps")
        et_ready = sem("et_ready")
        agg_done = sem("agg_done")
        u_done = sem("u_done")
        st1_ready = sem("st1_ready")
        mv1_ready = sem("mv1_ready")
        ve1_ready = sem("ve1_ready")
        rs1_ready = sem("rs1_ready")
        z_ready = sem("z_ready")
        h_scaled = sem("h_scaled")
        h_ready = sem("h_ready")
        zt_ps = sem("zt_ps")
        zt_hi_ready = sem("zt_hi_ready")
        zt_lo_ready = sem("zt_lo_ready")
        ff1_done = sem("ff1_done")
        g_hi_ready = sem("g_hi_ready")
        gelu_done = sem("gelu_done")
        g_lo_ready = sem("g_lo_ready")
        g_lo_pool = sem("g_lo_pool")
        ff2_done = sem("ff2_done")
        v_done = sem("v_done")
        st2_ready = sem("st2_ready")
        mv2_ready = sem("mv2_ready")
        ve2_ready = sem("ve2_ready")
        rs2_ready = sem("rs2_ready")
        z2_ready = sem("z2_ready")
        xo_scaled = sem("xo_scaled")
        xo_shifted = sem("xo_shifted")
        xo_ready = sem("xo_ready")

        masks0_ready = sem("masks0_ready")
        dots0_ready = sem("dots0_ready")
        scores0_ready = sem("scores0_ready")
        max0_steps = sem("max0_steps")
        cc0_ready = sem("cc0_ready")
        e12_0_ready = sem("e12_0_ready")
        e0_ready = sem("e0_ready")
        rinv0_ready = sem("rinv0_ready")
        et0_ps = sem("et0_ps")
        et0_ready = sem("et0_ready")
        agg0_done = sem("agg0_done")
        elu_parts = sem("elu_parts")
        elu_sum = sem("elu_sum")
        x1_ready = sem("x1_ready")
        st3_ready = sem("st3_ready")
        mv3_ready = sem("mv3_ready")
        ve3_ready = sem("ve3_ready")
        rs3_ready = sem("rs3_ready")
        nm3_ready = sem("nm3_ready")
        x_made = sem("x_made")
        st4_ready = sem("st4_ready")
        mv4_ready = sem("mv4_ready")
        ve4_ready = sem("ve4_ready")
        rs4_ready = sem("rs4_ready")
        nm4_ready = sem("nm4_ready")
        h0_ready = sem("h0_ready")

        def live(u):
            return 0 <= u < U

        def early_step(v):
            return v - FILL if v < CH else 2 + L * (v - CH)

        stage_of = {early_step(v) + j: {} for v in range(G) for j in range(4)}
        for v in range(G):
            for j in range(4):
                stage_of[early_step(v) + j][j] = v

        def early(s):
            return stage_of.get(s, {}).get(0)

        def middle(s):
            return stage_of.get(s, {}).get(1)

        def late(s):
            return stage_of.get(s, {}).get(2)

        def end(s):
            return stage_of.get(s, {}).get(3)

        XO_IDLE = 5

        def ahead(v):
            return v > CH

        def only_middle(s):
            return middle(s) is not None and early(s) is None and late(s) is None

        def residual_x(v):
            return xin[1] if v < CH else xin[0]

        def made(v):
            return xo if v < XO_IDLE else xin[1] if v < CH else h0[v % 2]

        POOL_LOW = (2, 5)

        def low_done(eng, st, s, c):
            own = [b for b in range(c + 1) if b in POOL_LOW]
            eng.wait_ge(g_lo_ready, st.nth(s, C - len(POOL_LOW), c + 1 - len(own)))
            if own:
                eng.wait_ge(g_lo_pool, st.nth(s, len(POOL_LOW), len(own)))

        def pick(units, st, u):
            if isinstance(st.off, int):
                return units[u]
            return units[bass.ds(st.off0 + u, 1)].rearrange("o n t d -> (o n) t d")

        def steps(eng, body, rest, s_rest):
            for s in range(-FILL, PER):
                if s == s_rest:
                    rest()
                body(Step(s))
            n = G // CH - 2
            with eng.Fori(0, n) as i:
                i = nc.s_assert_within(i, 0, n - 1, skip_runtime_bounds_check_because="the loop ends before n")
                for s in range(PER, 2 * PER):
                    body(Step(s, i * PER, i * CH))
            for s in range(U - PER, U + 2):
                body(Step(s))

        def all_graphs(row):
            return row.unsqueeze(1).to_broadcast((P, T, D))

        def affine(eng, st, u):
            l = layer(u)
            last = l == L - 1
            eng.wait_ge(z2_ready, st.nth(u))
            eng.tensor_tensor(xo[:, :, :], xo[:, :, :], all_graphs(g2_row[:, l, :]), ALU.mult).then_inc(xo_scaled, 1)
            eng.wait_ge(xo_scaled, st.nth(u))
            eng.tensor_tensor(xo[:, :, :], xo[:, :, :], all_graphs(beta2_row[:, l, :]),
                              ALU.add).then_inc(xo_shifted if last else xo_ready, 1)
            if last:
                eng.wait_ge(xo_shifted, st.nth0(group(u)))
                eng.wait_ge(r_in, 16 * st.nth0(group(u)))
                eng.tensor_tensor(xo[:, :, :], xo[:, :, :], xin[1][:, :, :], ALU.add).then_inc(xo_ready, 1)

        block = ctx.enter_context(nc.Block())

        @block.sync
        def _(sp):
            def spread(v):
                return v.partition_broadcast(P)

            sp.dma_start(a_col[:, :], w_attn0.rearrange("o (h k) -> k (o h)", h=2),
                         allow_slow_non_contiguous=True).then_inc(const_in, 16)
            sp.dma_start(wfc, w_fc).then_inc(const_in, 16)
            sp.dma_start(beta1_col[:, :, :], beta1.rearrange("l (k p) -> p l k", p=P),
                         allow_slow_non_contiguous=True).then_inc(const_in, 16)
            sp.dma_start(g1_col[:, :, :], g1.rearrange("l (k p) -> p l k", p=P),
                         allow_slow_non_contiguous=True).then_inc(const_in, 16)
            sp.dma_start(b1_col[:, :, :], b1.rearrange("l (c p) -> p l c", p=P),
                         allow_slow_non_contiguous=True).then_inc(const_in, 16)

            def raw_weights(l):
                if l >= 2:
                    sp.wait_ge(w_hi_ready, 2 * K1 * (l - 1))
                    sp.wait_ge(w_ready, 2 * K1 * (l - 1))
                    sp.wait_ge(b1_ps, l - 1)
                for k in range(K1):
                    sp.dma_start(raw1[l % 2][k].rearrange("p t d -> p (t d)"),
                                 w1[l, k * P:(k + 1) * P, :]).then_inc(w_in[l], 16)
                    sp.dma_start(raw2[l % 2][k][:, :, :], w2[l].rearrange("(c p) d -> p c d", p=P)[
                        :, k * HC:(k + 1) * HC, :]).then_inc(w_in[l], 16)

            def rest():
                raw_weights(2)
                sp.wait_ge(w_ready, 2 * K1 * 2)
                sp.wait_ge(w_hi_ready, 2 * K1 * 2)
                sp.dma_start(xo[:, 0:L, :], spread(b2)).then_inc(rows_in, 16)
                sp.dma_start(bb_row[:, :, :], spread(beta1)).then_inc(rows_in, 16)
                sp.dma_start(aw_row[:, :, :], spread(attn_w)).then_inc(rows_in, 16)
                sp.dma_start(ab_col[:, :], spread(attn_b)).then_inc(rows_in, 16)
                sp.dma_start(g1_row[:, :, :], spread(g1)).then_inc(rows_in, 16)
                sp.dma_start(g2_row[:, :, :], spread(g2)).then_inc(rows_in, 16)
                sp.dma_start(beta2_row[:, :, :], spread(beta2)).then_inc(rows_in, 16)

            raw_weights(0)
            raw_weights(1)

            def body(st):
                s = st.s
                v0, v1, v2, v3 = early(s), middle(s), late(s), end(s)
                if v3 is not None and v3 < CH:
                    sp.wait_ge(x1_ready, st.nth0(v3))
                    sp.dma_start(pick(r_u, st, v3), elu_r[:, :, :]).then_inc(r_out, 16)
                if v0 is not None and not ahead(v0):
                    if v0:
                        sp.wait_ge(h0_ready, st.nth0(v0 - 1))
                    sp.dma_start(xin[0][:, :, :], pick(x_u, st, v0)).then_inc(xin_in, 16)
                if v2 is not None and v2 <= XO_IDLE:
                    if v2:
                        sp.wait_ge(x1_ready, st.nth0(v2 - 1))
                    sp.dma_start(xin[1][:, :, :], pick(x_u, st, v2)).then_inc(xr_in, 16)
                if s == -3:
                    sp.wait_ge(w_hi_ready, 2 * K1 * L)
                    sp.wait_ge(w_ready, 2 * K1 * L)
                    sp.wait_ge(b1_ps, L)
                if live(s + 3):
                    if live(s + 2):
                        sp.wait_ge(scores_ready, st.nth(s + 2))
                    sp.dma_start(m1[(s + 3) % 2][:, :, :].bitcast(I32), pick(m_u, st, group(s + 3))).then_inc(m_in, 16)
                    if layer(s + 3) == 0 and (group(s + 3) < CH or group(s + 3) == G - 1):
                        sp.wait_ge(h_out, 16 * st.nth0(group(s + 3)))
                    if live(s + 1):
                        sp.wait_ge(u_done, st.nth(s + 1))
                    sp.dma_start(xb[(s + 3) % 2][:, :, :],
                                 pick(xs_u, st, layer(s + 3) * G + group(s + 3))).then_inc(x_in, 16)
                if live(s - 2):
                    if s >= PER and live(s + 4) and layer(s + 4) == 0 and group(s + 4) % CH == CH - 1:
                        sp.wait_ge(h_out, 16 * st.nth0(group(s + 4)))
                    sp.wait_ge(xo_ready, st.nth(s - 2))
                    l, g = layer(s - 2), group(s - 2)
                    dst = pick(out_u, st, g) if l == L - 1 else pick(xs_u, st, (l + 1) * G + g)
                    sp.dma_start(dst, xo[:, :, :]).then_inc(y_out, 16)
                if live(s - 1) and layer(s - 1) == L - 1:
                    sp.dma_start(xin[1][:, :, :], pick(r_u, st, group(s - 1))).then_inc(r_in, 16)
                if v0 is not None:
                    if live(s):
                        sp.wait_ge(g_lo_pool, st.nth(s, 2))
                    if v0:
                        sp.wait_ge(masks0_ready, st.nth0(v0 - 1))
                        sp.wait_ge(masks_sum, st.nth0(v0 - 1))
                    sp.dma_start(adj_i[:, :, :], pick(adj_u, st, v0)).then_inc(adj_in, 16)
                if v3 is not None:
                    sp.wait_ge(r_out, 16 * st.nth0(v3))
                    sp.wait_ge(m_out, 16 * st.nth0(v3))
                    sp.wait_ge(x_made, st.nth0(v3))
                    sp.dma_start(pick(xs_u, st, v3), made(v3)[:, :, :]).then_inc(h_out, 16)
                if v2 is not None and XO_IDLE < v2 < CH:
                    sp.wait_ge(h_out, 16 * st.nth0(v2 - 1))
                    sp.dma_start(xin[1][:, :, :], pick(x_u, st, v2)).then_inc(xr_in, 16)
                if v1 is not None:
                    sp.wait_ge(masks_ready, st.nth0(v1))
                    sp.dma_start(pick(m_u, st, v1), m_new[:, :, :].bitcast(I32)).then_inc(m_out, 16)
                if v2 is not None and v2 >= CH:
                    sp.wait_ge(x1_ready, st.nth0(v2))
                    sp.dma_start(pick(r_u, st, v2), elu_r[:, :, :]).then_inc(r_out, 16)
                v = early(s + 1)
                if v is not None and ahead(v):
                    sp.dma_start(xin[0][:, :, :], pick(x_u, st, v)).then_inc(xin_in, 16)

            steps(sp, body, rest, -FILL + 1)
            sp.wait_ge(y_out, 16 * U)
            sp.wait_ge(r_out, 16 * G)
            sp.wait_ge(h_out, 16 * G)
            sp.wait_ge(m_out, 16 * G)

        @block.tensor
        def _(pe):
            pe.wait_ge(const_in, 16 * 5)
            for j in range(2):
                mm = pe.matmul(ps_s[:, j * D:(j + 1) * D], a_col[:, j:j + 1].to_broadcast((O, P)), wfc,
                               start=True, stop=True)
            mm.then_inc(v_ps, 1)

            def bias_shift(l):
                pe.wait_ge(w_in[l], 16 * 2 * K1)
                if l == 2:
                    pe.wait_ge(b1_ready, 1)
                for c in range(C):
                    for k in range(K1):
                        mm = pe.matmul(bank[0][:, l * C + c:l * C + c + 1],
                                       raw1[l % 2][k].rearrange("p t d -> p (t d)")[:, c * P:(c + 1) * P],
                                       beta1_col[:, l, k:k + 1], start=(k == 0), stop=(k == K1 - 1))
                mm.then_inc(b1_ps, 1)

            bias_shift(0)
            bias_shift(1)
            pe.wait_ge(ident_ready, 2)

            def score_rows(scores, mask, dot, done):
                for t in range(T):
                    pe.matmul(scores[:, t * P:(t + 1) * P], dot[:, 1, t:t + 1].to_broadcast((P, P)), ident[:, :],
                              is_transpose=True, start=(t == 0), stop=True, skip_group_check=True)
                pe.matmul(scores[:, :], ident_b[:, :], mask.rearrange("p t m -> p (t m)"),
                          start=False, stop=True, skip_group_check=True).then_inc(done, 1)

            def bank_read(st, s, c):
                if c in POOL_LOW:
                    pe.wait_ge(gelu_done, st.nth(s, C, c + 1))
                else:
                    pe.wait_ge(g_lo_ready, st.nth(s, C - len(POOL_LOW), c + 1 - sum(b < c for b in POOL_LOW)))

            def turn_weights(dst, done):
                for t in range(T):
                    mm = pe.transpose(dst[:, t * P:(t + 1) * P], e1[:, t, :], ident[:, :])
                mm.then_inc(done, 1)

            def aggregate(weights, rows, done):
                for t in range(T):
                    pe.matmul(ps_u[t // 2][:, t % 2 * D:(t % 2 + 1) * D], weights[:, t, :], rows[:, t, :],
                              start=True, stop=True).then_inc(done, 1)

            def body(st):
                s = st.s
                v1, v2 = middle(s), late(s)
                l = layer(s)

                def hidden(c):
                    if not live(s):
                        return
                    if s == c == 0:
                        pe.wait_ge(w_hi_ready, 2 * K1 * L)
                        pe.wait_ge(w_ready, 2 * K1 * L)
                        pe.wait_ge(b1_ready, 2)
                    if c == 0:
                        pe.wait_ge(zt_hi_ready, st.nth(s, K1))
                        pe.wait_ge(zt_lo_ready, st.nth(s))
                    if bank[turn[c]] in ps_y and c < 4 and live(s - 1):
                        pe.wait_ge(v_done, st.nth(s - 1, 2, turn[c] - 1))
                    if c >= 4:
                        bank_read(st, s, turn[:4].index(turn[c]))
                    n = 0
                    for k in range(K1):
                        for w, z in ((w1_hi, zt_hi), (w1_hi, zt_lo), (w1_lo, zt_hi)):
                            mm = pe.matmul(bank[turn[c]][:, :], w[:, l, k, c * P:(c + 1) * P], z[:, k, :],
                                           start=(n == 0), stop=(n == 3 * K1 - 1))
                            n += 1
                    mm.then_inc(ff1_done, 1)

                def second(r):
                    if not live(s):
                        return
                    if r in (0, 2):
                        bank_read(st, s, 5 if r == 0 else 7)
                    for c in range(C):
                        if r == 0:
                            low_done(pe, st, s, c)
                        y = ps_y[r // 2][:, r % 2 * D:(r % 2 + 1) * D]
                        for n, (g, w) in enumerate(((g_hi, w2_hi), (g_hi, w2_lo), (g_lo, w2_hi))):
                            mm = pe.matmul(y, g[:, c, r * P:(r + 1) * P], w[:, l, c, :],
                                           start=(c == 0 and n == 0), stop=(c == C - 1 and n == 2))
                    mm.then_inc(ff2_done, 1)

                hidden(0)
                if live(s + 1):
                    pe.wait_ge(et_ready, st.nth(s + 1))
                    if late(s - 1) is not None:
                        pe.wait_ge(elu_parts, st.nth0(late(s - 1)))
                    if live(s):
                        pe.wait_ge(zt_lo_ready, st.nth(s))
                    aggregate(et, xb[(s + 1) % 2], agg_done)
                hidden(1)
                if live(s + 2):
                    pe.wait_ge(dots_ready, st.nth(s + 2, 2 * T))
                    pe.wait_ge(m_in, 16 * st.nth(s + 2))
                    if live(s + 1):
                        pe.wait_ge(et_ready, st.nth(s + 1))
                    score_rows(ps_s, m1[s % 2][:, :, :], dots[s % 2], scores_ready)
                if v2 is not None:
                    pe.wait_ge(e0_ready, st.nth0(v2))
                    turn_weights(ps_s0, et0_ps)
                hidden(2)
                hidden(3)
                if v1 is not None:
                    pe.wait_ge(dots0_ready, st.nth0(v1, 2 * T))
                    pe.wait_ge(masks0_ready, st.nth0(v1))
                    if v1:
                        pe.wait_ge(et0_ready, st.nth0(v1 - 1))
                    score_rows(ps_s0, m0[:, :, :], dots0, scores0_ready)
                for c in range(4, C):
                    hidden(c)
                if live(s + 1):
                    pe.wait_ge(z_ready, st.nth(s + 1))
                    for k in range(K1):
                        for t in range(T):
                            mm = pe.transpose(ps_u[k][:, t * P:(t + 1) * P], ub[:, t, k * P:(k + 1) * P], ident[:, :])
                    mm.then_inc(zt_ps, 1)
                second(0)
                second(1)
                if v2 is not None:
                    pe.wait_ge(et0_ready, st.nth0(v2))
                    if live(s + 1):
                        pe.wait_ge(zt_lo_ready, st.nth(s + 1))
                    elif late(s - 1) is not None:
                        pe.wait_ge(elu_parts, st.nth0(late(s - 1)))
                    aggregate(et0, h0[v2 % 2], agg0_done)
                second(2)
                if live(s + 2):
                    pe.wait_ge(e_ready, st.nth(s + 2))
                    turn_weights(ps_s, et_ps)
                second(3)

            steps(pe, body, lambda: bias_shift(2), -FILL + 2)

        @block.scalar
        def _(act):
            def high_halves(l):
                act.wait_ge(w_in[l], 16 * 2 * K1)
                for k in range(K1):
                    act.activation(w1_hi[:, l, k, :], raw1[l % 2][k].rearrange("p t d -> p (t d)"), ACT.Copy,
                                   scale=g1_col[:, l, k:k + 1]).then_inc(w_hi_ready, 1)
                    act.activation(w2_hi[:, l, k * HC:(k + 1) * HC, :], raw2[l % 2][k][:, :, :],
                                   ACT.Copy).then_inc(w_hi_ready, 1)

            act.wait_ge(const_in, 16 * 5)
            high_halves(0)
            high_halves(1)
            act.wait_ge(w_ready, 2 * K1 * 2)
            act.wait_ge(b1_ready, 1)

            def exps(scores, cols):
                for t in range(T):
                    src = scores[:, t * P:(t + 1) * P]
                    act.activation(e1[:, t, :], src, ACT.Exp, bias=cols[:, 0, t:t + 1])
                    a = act.activation(e2[:, t, :], src, ACT.Exp, bias=cols[:, 1, t:t + 1], scale=SLOPE)
                return a

            def norm_relu(dst, src, rs, nm):
                for t in range(T):
                    a = act.activation(dst[:, t, :], src[:, t, :], ACT.Relu, bias=nm[:, t:t + 1], scale=rs[:, t:t + 1])
                return a

            def body(st):
                s = st.s
                v0, v1, v2, v3 = early(s), middle(s), late(s), end(s)

                def turned0():
                    if v2 is not None:
                        act.wait_ge(et0_ps, st.nth0(v2))
                        if v2:
                            act.wait_ge(agg0_done, st.nth0(v2 - 1, T))
                        act.activation(et0.rearrange("p t m -> p (t m)"), ps_s0[:, :], ACT.Copy).then_inc(et0_ready, 1)

                if live(s):
                    for c in range(C):
                        act.wait_ge(ff1_done, st.nth(s, C, c + 1))
                        block_in = bank[turn[c]][:, :]
                        bias = b1_eff[:, layer(s), c:c + 1]
                        act.activation(g_hi[:, c, :], block_in, ACT.Gelu, bias=bias).then_inc(g_hi_ready, 1)
                        if c not in POOL_LOW:
                            act.wait_ge(g_hi_ready, st.nth(s, C, c + 1))
                            full = block_in
                        else:
                            full = g_full
                            if c == POOL_LOW[0] and early(s - 1) is not None:
                                act.wait_ge(masks0_ready, st.nth0(early(s - 1)))
                                act.wait_ge(masks_sum, st.nth0(early(s - 1)))
                            elif c == POOL_LOW[1]:
                                act.wait_ge(g_lo_pool, st.nth(s, 2, 1))
                        act.activation(full, block_in, ACT.Gelu, bias=bias).then_inc(gelu_done, 1)
                        if c == 1:
                            turned0()
                else:
                    turned0()
                if live(s + 1):
                    act.wait_ge(zt_ps, st.nth(s + 1))
                    for k in range(K1):
                        act.activation(zt_hi[:, k, :], ps_u[k][:, :], ACT.Copy).then_inc(zt_hi_ready, 1)
                if live(s + 2):
                    act.wait_ge(cc_ready, st.nth(s + 2))
                    exps(ps_s, cc).then_inc(e12_ready, 1)
                if v3 is not None:
                    act.wait_ge(nm3_ready, st.nth0(v3))
                    norm_relu(made(v3), elu_r, rs3, nm3).then_inc(x_made, 1)
                if v2 is not None:
                    act.wait_ge(rinv0_ready, st.nth0(v2))
                    if v2:
                        act.wait_ge(r_out, 16 * st.nth0(v2 - 1))
                        act.wait_ge(x_made, st.nth0(v2 - 1))
                    if live(s - 1):
                        act.wait_ge(z2_ready, st.nth(s - 1))
                    for t in range(T):
                        if t % 2 == 0:
                            act.wait_ge(agg0_done, st.nth0(v2, T, t + 2))
                        src = ps_u[t // 2][:, t % 2 * D:(t % 2 + 1) * D]
                        act.activation(elu_e[:, t, :], src, ACT.Exp, scale=rinv0[:, t:t + 1])
                        a = act.activation(elu_r[:, t, :], src, ACT.Relu, scale=rinv0[:, t:t + 1])
                    a.then_inc(elu_parts, 1)
                if live(s + 2):
                    act.wait_ge(et_ps, st.nth(s + 2))
                    if live(s + 1):
                        act.wait_ge(agg_done, st.nth(s + 1, T))
                    act.activation(et.rearrange("p t m -> p (t m)"), ps_s[:, :], ACT.Copy).then_inc(et_ready, 1)
                if v0 is not None:
                    act.wait_ge(nm4_ready, st.nth0(v0))
                    if v0 >= 2:
                        act.wait_ge(agg0_done, st.nth0(v0 - 2, T))
                    if v0 >= CH + 2:
                        act.wait_ge(h_out, 16 * st.nth0(v0 - 2))
                    norm_relu(h0[v0 % 2], xin[0], rs4, nm4).then_inc(h0_ready, 1)
                if v1 is not None:
                    act.wait_ge(cc0_ready, st.nth0(v1))
                    if live(s + 2):
                        act.wait_ge(et_ps, st.nth(s + 2))
                    exps(ps_s0, cc0).then_inc(e12_0_ready, 1)

            steps(act, body, lambda: high_halves(2), -FILL + 2)

        @block.vector
        def _(dve):
            done = [0]

            def link(ins):
                done[0] += 1
                ins.then_inc(pro, 1)
                dve.wait_ge(pro, done[0])

            link(dve.memset(neg_half[:, :], -0.5))
            dve.wait_ge(const_in, 16 * 5)
            dve.wait_ge(v_ps, 1)
            link(dve.tensor_copy(v_row.rearrange("p a d -> p (a d)"), ps_s[:, :]))

            def low_halves(l):
                dve.wait_ge(w_in[l], 16 * 2 * K1)
                for k in range(K1):
                    dve.wait_ge(w_hi_ready, 2 * (K1 * l + k) + 1)
                    dve.scalar_tensor_tensor(out=w1_lo[:, l, k, :], in0=raw1[l % 2][k].rearrange("p t d -> p (t d)"),
                                             scalar=g1_col[:, l, k:k + 1], in1=w1_hi[:, l, k, :].bitcast(F32),
                                             op0=ALU.mult, op1=ALU.subtract).then_inc(w_ready, 1)
                    dve.wait_ge(w_hi_ready, 2 * (K1 * l + k) + 2)
                    dve.tensor_tensor(w2_lo[:, l, k * HC:(k + 1) * HC, :], raw2[l % 2][k][:, :, :],
                                      w2_hi[:, l, k * HC:(k + 1) * HC, :].bitcast(F32),
                                      ALU.subtract).then_inc(w_ready, 1)

            def biases(l0, l1):
                dve.wait_ge(b1_ps, l1)
                dve.tensor_tensor(b1_eff[:, l0:l1, :].rearrange("p l c -> p (l c)"), bank[0][:, l0 * C:l1 * C],
                                  b1_col[:, l0:l1, :].rearrange("p l c -> p (l c)"), ALU.add).then_inc(b1_ready, 1)

            def rest():
                low_halves(2)
                biases(2, L)
                dve.wait_ge(rows_in, 16 * 7)
                link(dve.tensor_tensor(bb_row[:, :, :], bb_row[:, :, :], xo[:, 0:L, :], ALU.add))

            dve.wait_ge(ident_ready, 3)
            low_halves(0)
            low_halves(1)
            biases(0, 2)

            def branch_biases(nth, u, scores, sm, dot, cols, per_head, steps_sem, ready):
                dve.tensor_reduce(sm[:, 0, :], scores.rearrange("p (t m) -> p t m", t=T), AX, ALU.max)
                if per_head is None:
                    dve.tensor_copy(sm[:, 1, :], dot[:, 0, :]).then_inc(steps_sem, 1)
                else:
                    dve.tensor_scalar(sm[:, 1, :], dot[:, 0, :], per_head, None, ALU.add).then_inc(steps_sem, 1)
                dve.wait_ge(steps_sem, nth(u, 3, 1))
                dve.tensor_tensor(sm[:, 2, :], sm[:, 0, :], sm[:, 1, :], ALU.add).then_inc(steps_sem, 1)
                dve.wait_ge(steps_sem, nth(u, 3, 2))
                dve.scalar_tensor_tensor(out=sm[:, 3, :], in0=sm[:, 2, :], scalar=SLOPE, in1=sm[:, 2, :],
                                         op0=ALU.mult, op1=ALU.max).then_inc(steps_sem, 1)
                dve.wait_ge(steps_sem, nth(u, 3, 3))
                dve.tensor_tensor(cols[:, 0, :], sm[:, 1, :], sm[:, 3, :], ALU.subtract)
                dve.scalar_tensor_tensor(out=cols[:, 1, :], in0=sm[:, 1, :], scalar=SLOPE, in1=sm[:, 3, :],
                                         op0=ALU.mult, op1=ALU.subtract).then_inc(ready, 1)

            def weights(nth, u, rs, ri, e12, e_done, r_done):
                dve.wait_ge(e12, nth(u))
                for t in range(T):
                    ins = dve.scalar_tensor_tensor(out=e1[:, t, :], in0=e1[:, t, :], scalar=1.0, in1=e2[:, t, :],
                                                   op0=ALU.mult, op1=ALU.max, accum_out=rs[:, t:t + 1])
                ins.then_inc(e_done, 1)
                dve.wait_ge(e_done, nth(u))
                dve.reciprocal(ri[:, :], rs[:, :]).then_inc(r_done, 1)

            def row_dots(nth, u, dot, rows, vec, ready, graphs=range(T)):
                for t in graphs:
                    for j in range(2):
                        if t:
                            dve.wait_ge(ready, nth(u, 2 * T, 2 * t + j - 1))
                        dve.tensor_tensor_reduce(junk[:, j, :], rows[:, t, :], vec(j), 1.0, 0.0,
                                                 ALU.mult, ALU.add, dot[:, j, t:t + 1]).then_inc(ready, 1)

            def statistics(rows, st_t, ready):
                for t in range(T):
                    ins = dve.bn_stats(st_t[:, t, :], rows[:, t, :])
                ins.then_inc(ready, 1)

            def variance(nth, u, st_t, mv, ve, mv_ready, ve_ready):
                for t in range(T):
                    ins = dve.bn_aggr(mv[:, t, :], st_t[:, t, :])
                ins.then_inc(mv_ready, 1)
                dve.wait_ge(mv_ready, nth(u))
                dve.tensor_scalar(ve[:, :], mv[:, :, 1], EPS, None, ALU.add).then_inc(ve_ready, 1)

            def normalise(dst, rows, mv, rs, ready):
                for t in range(T):
                    ins = dve.tensor_scalar(dst[:, t, :], rows[:, t, :], mv[:, t, 0:1], rs[:, t:t + 1],
                                            ALU.subtract, ALU.mult)
                ins.then_inc(ready, 1)

            def body(st):
                s = st.s
                v0, v1, v2, v3 = early(s), middle(s), late(s), end(s)

                def g_low(c):
                    if live(s) and c not in POOL_LOW:
                        dve.wait_ge(gelu_done, st.nth(s, C, c + 1))
                        dve.tensor_tensor(g_lo[:, c, :], bank[turn[c]][:, :], g_hi[:, c, :].bitcast(F32),
                                          ALU.subtract).then_inc(g_lo_ready, 1)

                def first_biases():
                    if v1 is not None:
                        dve.wait_ge(scores0_ready, st.nth0(v1))
                        branch_biases(st.nth0, v1, ps_s0, small0, dots0, cc0, None, max0_steps, cc0_ready)

                def second_statistics():
                    if live(s - 1):
                        dve.wait_ge(v_done, st.nth(s - 1, 2))
                        statistics(vb, st2, st2_ready)
                        dve.wait_ge(st2_ready, st.nth(s - 1))

                def second_variance():
                    if live(s - 1):
                        variance(st.nth, s - 1, st2, mv2, ve2, mv2_ready, ve2_ready)

                def second_normalise():
                    if live(s - 1):
                        dve.wait_ge(rs2_ready, st.nth(s - 1))
                        if live(s - 2):
                            dve.wait_ge(y_out, 16 * st.nth(s - 2))
                        else:
                            dve.wait_ge(h_out, 16 * XO_IDLE)
                        normalise(xo, vb, mv2, rs2, z2_ready)

                def input_statistics():
                    dve.wait_ge(xin_in, 16 * st.nth0(v0))
                    statistics(xin[0], st4, st4_ready)
                    dve.wait_ge(st4_ready, st.nth0(v0))

                def input_variance():
                    variance(st.nth0, v0, st4, mv4, ve4, mv4_ready, ve4_ready)

                def input_shift():
                    dve.wait_ge(rs4_ready, st.nth0(v0))
                    dve.scalar_tensor_tensor(out=nm4[:, :], in0=mv4[:, :, 0], scalar=-1.0, in1=rs4[:, :],
                                             op0=ALU.mult, op1=ALU.mult).then_inc(nm4_ready, 1)

                if live(s - 1):
                    dve.wait_ge(h_ready, st.nth(s - 1))
                    if live(s - 2):
                        dve.wait_ge(z2_ready, st.nth(s - 2))
                    if late(s - 1) is not None:
                        dve.wait_ge(x1_ready, st.nth0(late(s - 1)))
                    for r in range(2):
                        dve.wait_ge(ff2_done, st.nth(s - 1, T, 2 * r + 2))
                        dve.tensor_tensor(vb[:, 2 * r:2 * r + 2, :], ps_y[r].rearrange("p (t d) -> p t d", d=D),
                                          hb[(s - 1) % 2][:, 2 * r:2 * r + 2, :], ALU.add).then_inc(v_done, 1)
                g_low(0)
                if live(s + 1):
                    dve.wait_ge(rinv_ready, st.nth(s + 1))
                    if live(s):
                        dve.wait_ge(h_ready, st.nth(s))
                        dve.wait_ge(zt_ps, st.nth(s))
                    if live(s + 2):
                        dve.wait_ge(dots_ready, st.nth(s + 2, 2 * T))
                    if early(s - 1) is not None:
                        dve.wait_ge(dots0_ready, st.nth0(early(s - 1), 2 * T))
                    for t in range(T):
                        if t % 2 == 0:
                            dve.wait_ge(agg_done, st.nth(s + 1, T, t + 2))
                        ins = dve.scalar_tensor_tensor(
                            out=ub[:, t, :], in0=ps_u[t // 2][:, t % 2 * D:(t % 2 + 1) * D],
                            scalar=rinv[:, t:t + 1], in1=xb[(s + 1) % 2][:, t, :], op0=ALU.mult, op1=ALU.add)
                    ins.then_inc(u_done, 1)
                    dve.wait_ge(u_done, st.nth(s + 1))
                    statistics(ub, st1, st1_ready)
                    dve.wait_ge(st1_ready, st.nth(s + 1))
                g_low(1)
                if live(s + 1):
                    variance(st.nth, s + 1, st1, mv1, ve1, mv1_ready, ve1_ready)
                if live(s + 2):
                    dve.wait_ge(scores_ready, st.nth(s + 2))
                    if live(s + 1):
                        dve.wait_ge(e12_ready, st.nth(s + 1))
                    l2 = layer(s + 2)
                    branch_biases(st.nth, s + 2, ps_s, small, dots[s % 2], cc, ab_col[:, l2:l2 + 1], max_steps, cc_ready)
                g_low(3)
                if live(s + 1):
                    dve.wait_ge(rs1_ready, st.nth(s + 1))
                    normalise(ub, ub, mv1, rs1, z_ready)
                g_low(4)
                if not only_middle(s):
                    second_statistics()
                g_low(6)
                if not only_middle(s):
                    second_variance()
                g_low(7)
                if v3 is not None:
                    dve.wait_ge(rs3_ready, st.nth0(v3))
                    dve.scalar_tensor_tensor(out=nm3[:, :], in0=mv3[:, :, 0], scalar=-1.0, in1=rs3[:, :],
                                             op0=ALU.mult, op1=ALU.mult).then_inc(nm3_ready, 1)
                if v0 is not None:
                    input_statistics()
                if live(s + 1):
                    for k in range(K1):
                        dve.wait_ge(zt_hi_ready, st.nth(s + 1, K1, k + 1))
                        ins = dve.tensor_tensor(zt_lo[:, k, :], ps_u[k][:, :], zt_hi[:, k, :].bitcast(F32),
                                                ALU.subtract)
                    ins.then_inc(zt_lo_ready, 1)
                if v0 is not None:
                    input_variance()
                if only_middle(s):
                    second_statistics()
                    first_biases()
                    second_variance()
                else:
                    second_normalise()
                if live(s + 2):
                    weights(st.nth, s + 2, rsum, rinv, e12_ready, e_ready, rinv_ready)
                if not only_middle(s):
                    first_biases()
                if live(s + 3):
                    dve.wait_ge(x_in, 16 * st.nth(s + 3))
                    if live(s + 1):
                        dve.wait_ge(h_scaled, st.nth(s + 1))
                        dve.wait_ge(zt_ps, st.nth(s + 1))
                    l3 = layer(s + 3)
                    row_dots(st.nth, s + 3, dots[(s + 3) % 2], xb[(s + 3) % 2],
                             lambda j: aw_row[:, l3, j * D:(j + 1) * D], dots_ready, range(T // 2))
                if v0 is not None:
                    input_shift()
                if live(s + 3):
                    row_dots(st.nth, s + 3, dots[(s + 3) % 2], xb[(s + 3) % 2],
                             lambda j: aw_row[:, l3, j * D:(j + 1) * D], dots_ready, range(T // 2, T))
                if v2 is not None:
                    dve.wait_ge(elu_parts, st.nth0(v2))
                    dve.scalar_tensor_tensor(out=elu_e.rearrange("p t d -> p (t d)"),
                                             in0=elu_e.rearrange("p t d -> p (t d)"), scalar=1.0,
                                             in1=elu_r.rearrange("p t d -> p (t d)"),
                                             op0=ALU.min, op1=ALU.add).then_inc(elu_sum, 1)
                    dve.wait_ge(elu_sum, st.nth0(v2))
                    if v2 < CH:
                        dve.wait_ge(xr_in, 16 * st.nth0(v2))
                    dve.scalar_tensor_tensor(out=elu_r.rearrange("p t d -> p (t d)"),
                                             in0=elu_e.rearrange("p t d -> p (t d)"), scalar=-1.0,
                                             in1=residual_x(v2).rearrange("p t d -> p (t d)"),
                                             op0=ALU.add, op1=ALU.add).then_inc(x1_ready, 1)
                    dve.wait_ge(x1_ready, st.nth0(v2))
                    statistics(elu_r, st3, st3_ready)
                    dve.wait_ge(st3_ready, st.nth0(v2))
                    dve.tensor_copy(small0[:, 4, :], neg_half[:, :])
                    variance(st.nth0, v2, st3, mv3, ve3, mv3_ready, ve3_ready)
                if only_middle(s):
                    second_normalise()
                if v1 is not None:
                    weights(st.nth0, v1, rsum0, rinv0, e12_0_ready, e0_ready, rinv0_ready)
                if v0 is not None:
                    dve.wait_ge(h0_ready, st.nth0(v0))
                    if live(s + 3):
                        dve.wait_ge(dots_ready, st.nth(s + 3, 2 * T))
                    row_dots(st.nth0, v0, dots0, h0[v0 % 2], lambda j: v_row[:, j, :], dots0_ready)
                    dve.wait_ge(adj_in, 16 * st.nth0(v0))
                    if v0:
                        dve.wait_ge(m_out, 16 * st.nth0(v0 - 1))
                    dve.tensor_tensor(m_new[:, :, :], adj_i[:, :, :], eye_i[:, :].unsqueeze(1).to_broadcast((P, T, P)),
                                      ALU.add).then_inc(masks_sum, 1)
                if s - 2 == U - 1:
                    affine(dve, st, s - 2)

            steps(dve, body, rest, -FILL + 2)

        @block.gpsimd
        def _(pool):
            pool.memset(ident[:, :], 0.0).then_inc(zeroed, 1)
            pool.memset(ident_b[:, :], 0.0).then_inc(zeroed, 1)
            pool.wait_ge(zeroed, 2)
            for m in (ident, ident_b):
                pool.affine_select(out=m[:, :], in_=m[:, :], compare_op=ALU.not_equal, fill=1.0, base=0,
                                   pattern=[[-1, P]], channel_multiplier=1).then_inc(ident_ready, 1)
            pool.wait_ge(ident_ready, 2)
            pool.tensor_copy(eye_i[:, :], ident[:, :]).then_inc(ident_ready, 1)
            pool.wait_ge(ident_ready, 3)

            def take_waits(j):
                pool.tensor_tensor(spare[:, j:j + 1], neg_half[:, 0:1], neg_half[:, 0:1], ALU.mult)

            def inverse_root(value, ve, rs, ve_ready, rs_ready):
                pool.wait_ge(ve_ready, value)
                pool.tensor_tensor(rs[:, :], ve[:, :], neg_half[:, :], ALU.pow).then_inc(rs_ready, 1)

            def body(st):
                s = st.s
                v0, v1, v2 = early(s), middle(s), late(s)
                if live(s - 2) and s - 2 < U - 1:
                    affine(pool, st, s - 2)
                if live(s + 1):
                    inverse_root(st.nth(s + 1), ve1, rs1, ve1_ready, rs1_ready)
                if live(s):
                    for c in POOL_LOW:
                        pool.wait_ge(gelu_done, st.nth(s, C, c + 1))
                        pool.tensor_tensor(g_lo[:, c, :], g_full, g_hi[:, c, :].bitcast(F32),
                                           ALU.subtract).then_inc(g_lo_pool, 1)
                if live(s + 1):
                    l = layer(s + 1)
                    pool.wait_ge(z_ready, st.nth(s + 1))
                    if live(s - 1):
                        pool.wait_ge(v_done, st.nth(s - 1, 2))
                    h = hb[(s + 1) % 2]
                    pool.tensor_tensor(h[:, :, :], ub[:, :, :], all_graphs(g1_row[:, l, :]), ALU.mult).then_inc(h_scaled, 1)
                if live(s - 1) and not only_middle(s):
                    inverse_root(st.nth(s - 1), ve2, rs2, ve2_ready, rs2_ready)
                if live(s + 1):
                    pool.wait_ge(h_scaled, st.nth(s + 1))
                    pool.tensor_tensor(h[:, :, :], h[:, :, :], all_graphs(bb_row[:, l, :]), ALU.add).then_inc(h_ready, 1)
                if live(s - 1) and only_middle(s):
                    inverse_root(st.nth(s - 1), ve2, rs2, ve2_ready, rs2_ready)
                if v0 is not None:
                    inverse_root(st.nth0(v0), ve4, rs4, ve4_ready, rs4_ready)
                if v1 is not None:
                    pool.wait_ge(masks_sum, st.nth0(v1))
                    take_waits(1)
                    pool.tensor_scalar(m_new[:, :, :], m_new[:, :, :], 0.0, -BIG,
                                       ALU.is_le, ALU.mult).then_inc(masks_ready, 1)
                if v0 is not None:
                    pool.wait_ge(adj_in, 16 * st.nth0(v0))
                    if v0:
                        pool.wait_ge(scores0_ready, st.nth0(v0 - 1))
                    take_waits(0)
                    pool.tensor_scalar(m0[:, :, :], adj_i[:, :, :], 0.0, -BIG,
                                       ALU.is_equal, ALU.mult).then_inc(masks0_ready, 1)
                if v2 is not None:
                    inverse_root(st.nth0(v2), ve3, rs3, ve3_ready, rs3_ready)

            steps(pool, body, lambda: None, -FILL + 1)


_INS = ["x", "adj", "L0_gnn_W_fc", "L0_gnn_W_attn", "L1_gnn_attn_w", "L1_gnn_attn_b", "L1_gnn_W1", "L1_gnn_b1",
        "L1_gnn_W2", "L1_gnn_b2", "L1_gnn_g1", "L1_gnn_beta1", "L1_gnn_g2", "L1_gnn_beta2"]


def kernel(**inputs):
    import numpy as np
    import concourse.bacc as bacc
    from concourse import mybir as mb
    from concourse.bass_utils import run_bass_kernel_spmd

    nc = bacc.Bacc("TRN2", target_bir_lowering=False, num_devices=1, dynamic_dma_scratch_size=1024)
    arrays, args = {}, []
    for name in _INS:
        a = np.ascontiguousarray(inputs[name])
        arrays[f"in_{name}"] = a
        args.append(nc.dram_tensor(f"in_{name}", a.shape, mb.dt.from_np(a.dtype), kind="ExternalInput").ap())
    out = nc.dram_tensor("out", inputs["x"].shape, mb.dt.float32, kind="ExternalOutput").ap()
    build(nc, *args, out)
    r = run_bass_kernel_spmd(nc, [arrays], core_ids=[0])
    return r.results[0]["out"]
```
